# Optimizing a Trainium2 kernel written in Bass

```python
import numpy as np
import jax
import jax.numpy as jnp

def _softmax(x, axis=-1):
    return jax.nn.softmax(x, axis=axis)

def _gelu(x):
    return jax.nn.gelu(x, approximate=True)

def _silu(x):
    return jax.nn.silu(x)

def _sigmoid(x):
    return jax.nn.sigmoid(x)

def _layernorm(x, axis=-1, eps=1e-05):
    m = jnp.mean(x, axis=axis, keepdims=True)
    v = jnp.var(x, axis=axis, keepdims=True)
    return (x - m) / jnp.sqrt(v + eps)

def _scatter_add(tgt, idx, src, axis=0):
    return tgt.at[idx].add(src)

def _segment_sum(src, seg, n):
    return jax.ops.segment_sum(src, seg, n)
kernel_name = 'mk_adj_preln_d2_adj_r2_a668ec'

def setup_inputs(seed: int=0):
    np.random.seed(seed)
    _w = jnp.asarray

    def _rec_inputs():
        import jax
        import jax.numpy as jnp
        _gk = jax.random.key(seed)
        x = -0.000929 + 1 * jax.random.normal(jax.random.fold_in(_gk, 1), (4096, 128), jnp.float32)
        _w = (1.0 + jnp.arange(4096, dtype=jnp.float32)) ** (-0.5)
        _w = _w / _w.mean()
        _pij = jnp.clip(0.000976562 * _w[:, None] * _w[None, :], 0.0, 1.0)
        _a = jax.random.uniform(jax.random.fold_in(_gk, 2), (4096, 4096)) < _pij
        adj = _a.astype(jnp.int32)
        return (x, adj)
    x, adj = _rec_inputs()

    def _L0_gnn_setup():
        import jax
        import jax.numpy as jnp
        import numpy as np
        from jax import lax
        N = 4096
        F = 128
        CHUNK = 64
        key = jax.random.key(seed)
        kx, ka = jax.random.split(key)
        X = jax.random.normal(kx, (N, F), dtype=jnp.float32)
        adj = jax.random.randint(ka, (N, N), 0, 2, dtype=jnp.int32)
        return {'X': X, 'adj': adj}
    _L0_gnn_all = _L0_gnn_setup()
    _L0_gnn_in = {k: v for k, v in _L0_gnn_all.items() if k in ()}
    del _L0_gnn_all

    def _L1_gnn_setup():
        import jax, jax.numpy as jnp
        import numpy as np
        N = 4096
        IN = 128
        OUT = 128
        THR = 0.0001
        ALPHA = 0.2
        NEG = -1000000000.0
        key = jax.random.key(seed)
        k1, k2, k3, k4 = jax.random.split(key, 4)
        inp = jax.random.normal(k1, (N, IN), jnp.float32)
        W = jax.random.normal(k2, (IN, OUT), jnp.float32) * (1.414 * np.sqrt(2.0 / (IN + OUT)))
        a = jax.random.normal(k3, (2 * OUT, 1), jnp.float32) * (1.414 * np.sqrt(2.0 / (2 * OUT + 1)))
        adj = jax.random.randint(k4, (N, N), 0, 2, jnp.int32)
        return {'input': inp, 'W': W, 'a': a, 'adj': adj, 'M': N}
    _L1_gnn_all = _L1_gnn_setup()
    _L1_gnn_in = {k: v for k, v in _L1_gnn_all.items() if k in ('W', 'a')}
    del _L1_gnn_all
    return {'x': x, 'adj': adj, 'L1_gnn_W': _L1_gnn_in['W'], 'L1_gnn_a': _L1_gnn_in['a']}

def reference(x, adj, L1_gnn_W, L1_gnn_a):
    import jax
    import jax.numpy as jnp

    def _L0_gnn_ref(X, adj):
        import jax
        import jax.numpy as jnp
        import numpy as np
        from jax import lax
        N = 4096
        F = 128
        CHUNK = 64
        neg = jnp.finfo(X.dtype).min
        mask = adj != 0
        n, f = X.shape

        def body(_, mrows):
            vals = jnp.max(jnp.where(mrows[:, :, None], X[None, :, :], neg), axis=1)
            has_nbr = jnp.any(mrows, axis=1)
            return (None, jnp.where(has_nbr[:, None], vals, jnp.zeros((), X.dtype)))
        _, out = lax.scan(body, None, mask.reshape(n // CHUNK, CHUNK, n))
        return out.reshape(n, f)

    def _L1_gnn_ref(input, W, a, adj, M):
        import jax, jax.numpy as jnp
        import numpy as np
        N = 4096
        IN = 128
        OUT = 128
        THR = 0.0001
        ALPHA = 0.2
        NEG = -1000000000.0
        h = input @ W
        a_src = a[:OUT, 0]
        a_dst = a[OUT:, 0]
        e = jax.nn.leaky_relu((h[:M] @ a_src)[:, None] + (h @ a_dst)[None, :], negative_slope=ALPHA)
        valid = (adj[:M] > 0) & (h.sum(axis=1) != 0)[None, :]
        att = jax.nn.softmax(jnp.where(valid, e, NEG), axis=1)
        att = jnp.where(valid, att, 0.0)
        L = valid.sum(axis=1).astype(h.dtype)
        top = att.max(axis=1)
        attention = jnp.where(att >= THR, att, 0.0) * L[:, None]
        attention = jnp.where((top > THR)[:, None], attention, 0.0)
        h_prime = attention @ h
        return jax.nn.elu(h[:M] + h_prime)
    h = jnp.maximum(_layernorm(x, axis=-1), 0.0)
    x = x + _L0_gnn_ref(h, adj)
    h = jnp.maximum(_layernorm(x, axis=-1), 0.0)
    x = x + _L1_gnn_ref(h, L1_gnn_W, L1_gnn_a, adj, 4096)
    return x

_drawn_inputs = setup_inputs


def setup_inputs(seed=0):
    import zlib

    import numpy as np

    out = dict(_drawn_inputs(seed))
    spreads = {}
    factors = {}
    for name, (base, spread) in spreads.items():
        noise = np.random.default_rng([zlib.crc32(name.encode()), seed]).standard_normal(out[name].shape)
        drawn = base * np.exp(spread * noise) if base else spread * noise
        out[name] = jnp.asarray(drawn.astype(out[name].dtype))
    for name, factor in factors.items():
        out[name] = (out[name] * factor).astype(out[name].dtype)
    return out
```

```python
from contextlib import ExitStack

import concourse.bass as bass
from concourse import mybir

N, F, P = 4096, 128, 128
NT = N // P
SEG = 8
CPS = N // SEG // P
M8 = 8
HUB = 16
PIECES = 64
TG = (10, NT - 10)
T0G = (0, 10)
CAP = (104, 88)
CAP1 = (80, 88)
LIST = (32, 16)
LIST0 = 48
CH = 8
SLOTS = 13
RSLOTS = 4
ROW = 132
STAGES = 3
BANK = 512
EPS, ALPHA, THR, NEG, BIG = 1e-5, 0.2, 1e-4, -1e9, 3e38

DENSE = ("in", "score", "bc", "bc_act", "bc_dve", "masked", "exp", "att", "turned", "copied", "summed", "own", "out")

f32, f16, bf16, i32 = mybir.dt.float32, mybir.dt.float16, mybir.dt.bfloat16, mybir.dt.int32
ALU = mybir.AluOpType
ACT = mybir.ActivationFunctionType
X = mybir.AxisListType.X


def build(nc, x, adj, adj_t, w, a, out):
    t0 = nc.dram_tensor("h0_rows", [N, F], f32, kind="Internal").ap()
    t1 = nc.dram_tensor("h_rows", [N, ROW], f32, kind="Internal").ap()
    run = [nc.dram_tensor(f"running{g}", [P * CAP[g] + 1, F], f32, kind="Internal").ap() for g in range(2)]

    ctx = ExitStack()
    with ctx:
        def sb(name, shape, dt=f32):
            return ctx.enter_context(nc.sbuf_tensor(name, shape, dt))

        def sem(name):
            return ctx.enter_context(nc.semaphore(name))

        xs = sb("xs", [P, NT, F])
        G = sb("gathered", [P, SLOTS * CH, ROW])
        R = sb("running", [P, RSLOTS, CH, F])
        h0 = R[:, :, :, :].rearrange("p s e f -> p (s e) f")
        HB = sb("h_store", [P, NT * ROW])
        HT = HB[:, 0:N]
        HR = HB[:, :].rearrange("p (t c) -> p t c", c=ROW)
        arena = sb("arena", [P, 18432])
        stage = [arena[:, s * N:(s + 1) * N].bitcast(i32) for s in range(STAGES)]
        mask = [arena[:, 3 * N + s * N // 2:3 * N + (s + 1) * N // 2].bitcast(f16) for s in range(STAGES)]
        adjn = arena[:, 0:N].bitcast(i32)
        maskn = arena[:, N:N + N // 2].bitcast(f16)
        junk = arena[:, N + N // 2:2 * N]
        V = arena[:, 0:N]
        U = arena[:, N:2 * N]
        T = arena[:, 2 * N:3 * N]
        A = arena[:, 3 * N:4 * N].rearrange("p (t f) -> p t f", f=F)
        work = sb("work", [P, 2 * TG[1] * SEG * M8])
        attT = work[:, 0:2 * BANK].rearrange("p (b n) -> p b n", b=2)
        xn = work[:, 2 * BANK:2 * BANK + 4 * F].rearrange("p (k f) -> p k f", f=F)
        hTs = work[:, 2 * BANK + 4 * F:2 * BANK + 8 * F]
        KSZ = TG[1] * SEG * M8
        tmpk = work[:, KSZ:2 * KSZ]
        ident = sb("ident", [P, P])
        identh = sb("identh", [P, P], f16)
        diag = sb("diag", [P, CPS, P], f16)
        kcol = sb("kcol", [P, CPS])
        ones = sb("ones", [P, 1])
        rowmask = sb("rowmask", [P, 1])
        pcol = sb("pcol", [P, 2])
        offs = sb("offs", [P, SEG, M8])
        tnum = sb("tnum", [P, max(TG)])
        qv = sb("qv", [P, 8, max(CAP1)])
        K0 = qv[:, :, :].rearrange("p a b -> p (a b)")[:, 0:PIECES * M8]
        K = [sb("K0_", [P, TG[0], SEG * M8])[:, :, :],
             work[:, 0:KSZ].rearrange("p (t m) -> p t m", m=SEG * M8)]
        st = sb("st", [P, 2, SEG * M8])
        cnt = [sb(f"cnt{g}", [P, TG[g]]) for g in range(2)]
        pre = sb("pre", [P, max(TG)])
        L3W = (LIST0 + (TG[0] - 1) * LIST[0], TG[1] * LIST[1])
        L3 = [sb(f"L3_{g}", [P, L3W[g]]) for g in range(2)]
        Q = [sb(f"Q{g}", [P, CAP[g]]) for g in range(2)]
        qi = sb("qi", [P, max(CAP)], i32)
        pad = sb("pad", [P, max(CAP)], i32)
        idx = [sb(f"idx{g}", [P, CAP[g]], i32) for g in range(2)]
        ti = sb("ti", [P, max(CAP)], i32)
        tf = [sb(f"tf{g}", [P, CAP[g]]) for g in range(2)]
        cont = [sb(f"cont{g}", [P, CAP[g]]) for g in range(2)]
        ef = sb("ef", [P, max(TG)])
        eidx = [sb(f"eidx{g}", [P, TG[g]], i32) for g in range(2)]
        nend = [sb(f"nend{g}", [P, CAP1[g]]) for g in range(2)]
        reset = [sb(f"reset{g}", [P, CAP1[g]]) for g in range(2)]
        nq = [sb(f"nq{g}", [P, CAP1[g]]) for g in range(2)]
        sgn = sb("sgn", [P, NT])
        ovs = sb("ovs", [P, 8])
        ovd = sb("ovd", [P, 2])
        flagf = sb("flagf", [1, 2])
        flag = sb("flag", [1, 1], i32)
        st6 = sb("st6", [P, NT, 6])
        mv = sb("mv", [P, NT, 2])
        sd = sb("sd", [P, NT])
        rstd = sb("rstd", [P, NT])
        epsb = sb("epsb", [P, 1])
        hm = sb("hm", [P, 4])
        Ws = sb("Ws", [P, F])
        WT = sb("WT", [P, F])
        a2 = sb("a2", [P, 2])
        Wa = sb("Wa", [P, 2])
        S = sb("S", [P, NT])
        hsum = sb("hsum", [P, NT])
        tail_ = arena[:, 4 * N:]
        WG = tail_[:, 0:4 * F].rearrange("p (k f) -> p k f", f=F)
        aggT = tail_[:, 4 * F:4 * F + P]
        sq = [tail_[:, 5 * F + g * P:5 * F + g * P + CAP1[g]] for g in range(2)]
        wq = [tail_[:, 7 * F + g * P:7 * F + g * P + CAP1[g]] for g in range(2)]
        dn = sb("dn", [P, 12])
        zrow = sb("zrow", [1, F])
        onesr = sb("onesr", [P, max(CAP1)])
        qe = sb("qe", [P, max(CAP1)])
        ovt = sb("ovt", [P, 5])
        zv = [G[:, 4 * b:4 * b + 4, 0:F] for b in range(2)]
        ezv = [G[:, 8 + 4 * b:12 + 4 * b, 0:F] for b in range(2)]

        ps = [ctx.enter_context(nc.psum_tensor(f"ps{b}", [P, 4, BANK], f32)) for b in range(2)]

        x_in = sem("x_in"); w_in = sem("w_in")
        adj_in = [sem(f"adj_in{s}") for s in range(STAGES)]
        stage_used = sem("stage_used")
        mask_used = sem("mask_used")
        keys_ready = sem("keys_ready")
        keys_used = sem("keys_used")
        picked = sem("picked")
        consts = sem("consts"); consts2 = sem("consts2")
        dve = sem("dve")
        pool = sem("pool")
        stats0 = sem("stats0"); sd0 = sem("sd0"); rstd0 = sem("rstd0"); h0_ready = sem("h0_ready")
        t0_in = sem("t0_in")
        h0t_ready = sem("h0t_ready"); h0t_used = sem("h0t_used")
        queue_ready = sem("queue_ready")
        gath = [sem(f"gath{s}") for s in range(SLOTS)]
        chunk_used = sem("chunk_used")
        stored = [sem(f"stored{s}") for s in range(RSLOTS)]
        zrow_in = sem("zrow_in")
        ends = [[sem(f"ends{l}_{b}") for b in range(8)] for l in range(2)]
        adjn_in = sem("adjn_in"); maskn_ready = sem("maskn_ready")
        hubp = sem("hubp"); hub_used = sem("hub_used"); hub_done = sem("hub_done"); hub_t = sem("hub_t")
        flag_sum = sem("flag_sum"); flag_ready = sem("flag_ready"); diffs = sem("diffs")
        wprep = sem("wprep"); wprep_c = sem("wprep_c")
        var1 = sem("var1"); sd1 = sem("sd1"); xn_ready = sem("xn_ready"); xnt = sem("xnt"); ht_ready = sem("ht_ready")
        h_mm = sem("h_mm"); hr_copied = sem("hr_copied"); hr_ready = sem("hr_ready")
        t1_in = sem("t1_in")
        exq = sem("exq"); exq_done = sem("exq_done"); w_ready = sem("w_ready")
        wg_ready = sem("wg_ready"); wg_used = sem("wg_used")
        ds1 = {n: sem(f"d_{n}") for n in DENSE}
        gl0 = {n: sem(f"g0_{n}") for n in ("in", "mask", "p", "used", "own", "t", "done")}
        gl1 = {n: sem(f"g1_{n}") for n in DENSE}
        z_ready = sem("z_ready"); ez_ready = sem("ez_ready"); o_ready = sem("o_ready"); out_in = sem("out_in")

        passed_v = sem("passed_v"); passed_pe = sem("passed_pe")

        block = ctx.enter_context(nc.Block())

        adjt_v = adj_t.rearrange("(t p) n -> t p n", p=P)
        adj_v = adj.rearrange("(t p) n -> t p n", p=P)
        x_v = x.rearrange("(t p) f -> p t f", p=P)
        out_v = out.rearrange("(t p) f -> p t f", p=P)
        t0_v = t0.rearrange("(t p) f -> p t f", p=P)
        t1_v = t1.rearrange("(t p) c -> p t c", p=P)

        NCH0 = [CAP[g] // CH for g in range(2)]
        NCH1 = [CAP1[g] // CH for g in range(2)]
        CHUNKS = [(0, g, c) for g in range(2) for c in range(NCH0[g])] \
            + [(1, g, c) for g in range(2) for c in range(NCH1[g])]
        FIRST = {(l, g): CHUNKS.index((l, g, 0)) for l in range(2) for g in range(2)}
        L0CH = sum(NCH0)

        def slot(n):
            return n % SLOTS

        def gathered(n):
            return 16 * CH * (n // SLOTS + 1)

        def rstored(n):
            return 16 * (n // RSLOTS + 1)

        LOOP = NT - 2

        @block.sync
        def _(sp):
            sp.dma_start(xs[:, :, :], x_v).then_inc(x_in, 16)
            for t in range(2):
                sp.dma_start(stage[t], adjt_v[t]).then_inc(adj_in[t], 16)
            sp.dma_start(Ws[:, :], w).then_inc(w_in, 16)
            sp.dma_start(a2[:, :], a).then_inc(w_in, 16)
            with sp.Fori(0, LOOP // STAGES) as i:
                for k in range(STAGES):
                    s = (2 + k) % STAGES
                    sp.wait_ge(stage_used, i * STAGES + (k + 1))
                    sp.dma_start(stage[s], adjt_v[i * STAGES + (2 + k)]).then_inc(adj_in[s], 16)
            sp.wait_ge(stage_used, NT + 1)
            sp.wait_ge(mask_used, NT + 1)
            sp.dma_start(adjn, adj_v[0]).then_inc(adjn_in, 16)
            sp.wait_ge(consts2, 1)
            for g in range(2):
                sp.dma_start(run[g][P * CAP[g]:P * CAP[g] + 1, :], zrow[:, :]).then_inc(zrow_in, 16)

            def store_chunk(n):
                l, g, c = CHUNKS[n]
                sp.wait_ge(chunk_used, n + 1)
                dst = run[g][0:P * CAP[g], :].rearrange("(p q) f -> p q f", p=P)
                sp.dma_start(dst[:, c * CH:(c + 1) * CH, :], R[:, n % RSLOTS, :, :]).then_inc(stored[n % RSLOTS], 16)

            for n in range(L0CH):
                store_chunk(n)
            sp.wait_ge(flag_ready, 1)
            with sp.If(sp.value_load(flag[0:1, 0:1], min_val=0, max_val=1) > 0):
                with sp.Fori(0, NT) as t:
                    sp.wait_ge(gl0["done"], t + 1)
                    sp.dma_start(adjn, adj_v[t]).then_inc(gl0["in"], 16)
                sp.wait_ge(gl0["done"], NT + 1)
            for b in range(8):
                sp.wait_ge(hr_ready, b + 1)
                sp.dma_start(t1_v[:, 4 * b:4 * b + 4, :], HR[:, 4 * b:4 * b + 4, :]).then_inc(t1_in, 16)
            sp.dma_start(adjn, adj_v[0]).then_inc(ds1["in"], 16)
            for n in range(L0CH, len(CHUNKS)):
                store_chunk(n)
            with sp.If(sp.value_load(flag[0:1, 0:1], min_val=0, max_val=1) > 0):
                sp.wait_ge(ds1["out"], 2)
                with sp.Fori(0, NT) as t:
                    sp.wait_ge(gl1["out"], t + 1)
                    sp.dma_start(adjn, adj_v[t]).then_inc(gl1["in"], 16)
            for b in range(8):
                sp.wait_ge(o_ready, b + 1)
                sp.dma_start(out_v[:, 4 * b:4 * b + 4, :], xs[:, 4 * b:4 * b + 4, :]).then_inc(out_in, 16)
            sp.wait_ge(out_in, 16 * 8)

        @block.gpsimd
        def _(gp):
            own = [0]

            def step(ins):
                ins.then_inc(pool, 1)
                own[0] += 1
                return own[0]

            step(gp.memset(ident[:, :], 0.0))
            step(gp.iota(kcol[:, :], [[8 * P, CPS]], base=8, channel_multiplier=8, allow_small_or_imprecise_dtypes=True))
            step(gp.iota(rowmask[:, :], [[0, 1]], base=0, channel_multiplier=1, allow_small_or_imprecise_dtypes=True))
            for g in range(2):
                step(gp.iota(pcol[:, g:g + 1], [[0, 1]], base=-1, channel_multiplier=CAP[g],
                             allow_small_or_imprecise_dtypes=True))
            step(gp.iota(offs[:, :, :], [[1, SEG], [0, M8]], base=1 - SEG, channel_multiplier=0,
                         allow_small_or_imprecise_dtypes=True))
            step(gp.iota(tnum[:, :], [[1, max(TG)]], base=0, channel_multiplier=0, allow_small_or_imprecise_dtypes=True))
            step(gp.memset(ones[:, :], 1.0))
            step(gp.memset(onesr[:, :], 1.0))
            step(gp.memset(epsb[:, :], EPS))
            step(gp.memset(zrow[:, :], 0.0))
            n = own[0]
            gp.wait_ge(pool, n)
            step(gp.affine_select(out=ident[:, :], in_=ident[:, :], compare_op=ALU.not_equal, fill=1.0, base=0,
                                  pattern=[[-1, P]], channel_multiplier=1))
            n = step(gp.memset(G[:, :, :], 0.0))
            gp.wait_ge(pool, n)
            gp.sem_inc(consts, 1)
            gp.wait_ge(rstd0, 1)
            mean = mv[:, :, 0:1].to_broadcast([P, NT, F])
            gp.tensor_tensor(h0, xs[:, :, :], mean, ALU.subtract).then_inc(pool, 1); own[0] += 1
            gp.wait_ge(pool, own[0])
            step(gp.tensor_tensor(h0, h0, rstd[:, :, None].to_broadcast([P, NT, F]), ALU.mult))
            gp.wait_ge(pool, own[0])
            gp.tensor_scalar_max(h0, h0, 0.0).then_inc(h0_ready, 1)
            gp.wait_ge(h0_ready, 1)
            gp.dma_start(t0_v, h0).then_inc(t0_in, 16)
            gp.wait_ge(t0_in, 16)

            def gather_chunk(n):
                l, g, c = CHUNKS[n]
                if c == 0 and l == 0:
                    gp.wait_ge(queue_ready, g + 1)
                if n >= SLOTS:
                    gp.wait_ge(chunk_used, n - SLOTS + 1)
                for e in range(CH):
                    src, wide = (t0, F) if l == 0 else (t1, ROW)
                    gp.indirect_dma_start(
                        G[:, slot(n) * CH + e, 0:wide], None, src,
                        bass.IndirectOffsetOnAxis(ap=idx[g][:, c * CH + e:c * CH + e + 1], axis=0),
                        bounds_check=N - 1, oob_is_err=False).then_inc(gath[slot(n)], 16)

            def gather_ends(l):
                gp.wait_ge(zrow_in, 16 * 2)
                for g in range(2):
                    last = FIRST[l, g] + (NCH0, NCH1)[l][g] - 1
                    for n in range(last - RSLOTS + 1, last + 1):
                        gp.wait_ge(stored[n % RSLOTS], rstored(n))
                    for t in range(TG[g]):
                        if l == 1 and g == 0 and t == 0:
                            continue
                        tile = T0G[g] + t
                        gp.indirect_dma_start(
                            A[:, tile, :], None, run[g],
                            bass.IndirectOffsetOnAxis(ap=eidx[g][:, t:t + 1], axis=0),
                            bounds_check=P * CAP[g], oob_is_err=False).then_inc(ends[l][tile // 4], 16)

            for n in range(L0CH):
                gather_chunk(n)
            gather_ends(0)
            gp.wait_ge(t1_in, 16 * 8)
            for n in range(L0CH, len(CHUNKS)):
                gather_chunk(n)
            gather_ends(1)

        @block.scalar
        def _(act):
            act.wait_ge(consts, 1)
            act.wait_ge(stats0, 1)
            nc.scalar.activation(sd[:, :], mv[:, :, 1], ACT.Sqrt, bias=epsb[:, 0:1]).then_inc(sd0, 1)
            act.wait_ge(wprep, 1)
            nc.scalar.activation(WT[:, :], ps[1][:, 3, 0:P], ACT.Copy).then_inc(wprep_c, 1)
            act.wait_ge(wprep, 2)
            nc.scalar.activation(Wa[:, :], ps[1][:, 2, 0:2], ACT.Copy).then_inc(wprep_c, 1)

            act.sem_inc(stage_used, 1)
            for t in range(2):
                act.wait_ge(adj_in[t], 16)
                src = stage[t].rearrange("p (c i) -> p c i", i=P)
                dst = mask[t].rearrange("p (c i) -> p c i", i=P)
                if t == 0:
                    nc.scalar.activation(dst[:, :, 0:HUB], src[:, :, 0:HUB], ACT.Sign)
                    nc.scalar.activation(dst[:, :, HUB:P], src[:, :, HUB:P], ACT.Sign,
                                         accum_out=sgn[:, 0:1]).then_inc(stage_used, 1)
                else:
                    nc.scalar.activation(dst, src, ACT.Sign, accum_out=sgn[:, t:t + 1]).then_inc(stage_used, 1)
            with act.Fori(0, LOOP // STAGES) as i:
                for k in range(STAGES):
                    s = (2 + k) % STAGES
                    act.wait_ge(adj_in[s], i * 16 + (16 if s == 2 else 32))
                    act.wait_ge(mask_used, i * STAGES + (k + 1))
                    nc.scalar.activation(mask[s], stage[s], ACT.Sign,
                                         accum_out=sgn[:, bass.ds(i * STAGES + (2 + k), 1)]).then_inc(stage_used, 1)
            for b in range(8):
                act.wait_ge(h0t_ready, b + 1)
                nc.scalar.activation(HT[:, b * BANK:(b + 1) * BANK], ps[1][:, b % 4, :], ACT.Copy).then_inc(h0t_used, 1)

            for b in range(8):
                act.wait_ge(var1, b + 1)
                nc.scalar.activation(sd[:, 4 * b:4 * b + 4], mv[:, 4 * b:4 * b + 4, 1], ACT.Sqrt,
                                     bias=epsb[:, 0:1]).then_inc(sd1, 1)
                act.wait_ge(xnt, b + 1)
                nc.scalar.activation(hTs, ps[0][:, 0, :], ACT.Relu).then_inc(ht_ready, 1)
                act.wait_ge(h_mm, b + 1)
                for k in range(4):
                    t = 4 * b + k
                    nc.scalar.activation(HR[:, t, 0:F], ps[0][:, 1, k * F:(k + 1) * F], ACT.Copy,
                                         accum_out=hsum[:, t:t + 1]).then_inc(hr_copied, 1)

            def dense(sems, n):
                act.wait_ge(sems["score"], n + 1)
                for h in range(2):
                    act.wait_ge(sems["bc"], n * 2 + (h + 1))
                    nc.scalar.activation(U[:, h * 2048:(h + 1) * 2048], ps[0][:, :, :].rearrange("p b n -> p (b n)"),
                                         ACT.Identity, bias=dn[:, 0:1]).then_inc(sems["bc_act"], 1)
                act.wait_ge(sems["masked"], n + 1)
                nc.scalar.activation(U, U, ACT.Exp, bias=dn[:, 3:4], accum_out=dn[:, 4:5]).then_inc(sems["exp"], 1)
                for b in range(8):
                    act.wait_ge(sems["turned"], n * 8 + (b + 1))
                    act.wait_ge(sems["summed"], n * 8 + max(b, 1))
                    nc.scalar.activation(attT[:, b % 2, :], ps[0][:, b % 2, :], ACT.Copy).then_inc(sems["copied"], 1)

            def weigh(g):
                act.wait_ge(exq, 2 * g + 1)
                nc.scalar.activation(qv[:, 4, 0:CAP1[g]], qv[:, 4, 0:CAP1[g]], ACT.Exp)
                nc.scalar.activation(qv[:, 5, 0:CAP1[g]], qv[:, 5, 0:CAP1[g]], ACT.Exp).then_inc(exq_done, 1)
                act.wait_ge(w_ready, g + 1)
                for e in range(CAP1[g]):
                    k = sum(CAP1[:g]) + e
                    if k >= 4:
                        act.wait_ge(wg_used, k - 3)
                    n = FIRST[1, g] + e // CH
                    nc.scalar.activation(WG[:, k % 4, :], G[:, slot(n) * CH + e % CH, 0:F], ACT.Copy,
                                         scale=wq[g][:, e:e + 1]).then_inc(wg_ready, 1)

            dense(ds1, 0)
            weigh(0)
            weigh(1)
            act.wait_ge(flag_ready, 1)
            with act.If(act.value_load(flag[0:1, 0:1], min_val=0, max_val=1) > 0):
                with act.Fori(0, NT) as t:
                    dense(gl1, t)
            for b in range(8):
                act.wait_ge(z_ready, b + 1)
                nc.scalar.activation(ezv[b % 2], ezv[b % 2], ACT.Exp).then_inc(ez_ready, 1)

        @block.tensor
        def _(pe):
            pe.wait_ge(w_in, 32)
            pe.wait_ge(consts, 1)
            nc.tensor.transpose(ps[1][:, 3, 0:P], Ws[:, :], ident[:, :]).then_inc(wprep, 1)
            pe.wait_ge(wprep_c, 1)
            nc.tensor.matmul(ps[1][:, 2, 0:2], WT[:, :], a2[:, :], start=True, stop=True).then_inc(wprep, 1)
            pe.wait_ge(consts2, 1)

            pe.sem_inc(mask_used, 1)
            pe.sem_inc(ds1["summed"], 1)

            def keys(unit, s, seg):
                pe.wait_ge(keys_used, unit)
                for c in range(CPS):
                    col = (seg * CPS + c) * P
                    last = nc.tensor.matmul(ps[0][:, seg % 4, c * P:(c + 1) * P], mask[s][:, col:col + P],
                                            diag[:, c, :], start=True, stop=True)
                last.then_inc(keys_ready, 1)
                return last

            for t in range(2):
                pe.wait_ge(stage_used, t + 2)
                for seg in range(SEG):
                    keys(t * SEG + seg + 1, t, seg)
                pe.wait_ge(keys_ready, (t + 1) * SEG)
                pe.sem_inc(mask_used, 1)
            with pe.Fori(0, LOOP // STAGES) as i:
                for k in range(STAGES):
                    pe.wait_ge(stage_used, i * STAGES + (4 + k))
                    for seg in range(SEG):
                        keys(i * (STAGES * SEG) + ((2 + k) * SEG + seg + 1), (2 + k) % STAGES, seg)
                    pe.wait_ge(keys_ready, i * (STAGES * SEG) + (3 + k) * SEG)
                    pe.sem_inc(mask_used, 1)

            pe.wait_ge(h0_ready, 1)
            for b in range(8):
                if b >= 4:
                    pe.wait_ge(h0t_used, b - 3)
                for k in range(4):
                    last = nc.tensor.transpose(ps[1][:, b % 4, k * P:(k + 1) * P], h0[:, 4 * b + k, :], ident[:, :])
                last.then_inc(h0t_ready, 1)
            pe.wait_ge(h0t_used, 8)

            def hub_half(n, i, h, ready, used):
                pe.wait_ge(used, n + 1)
                row = identh[:, bass.ds(i, 1)].to_broadcast([P, P])
                for b in range(4):
                    last = nc.tensor.matmul(ps[h][:, b, :], row, maskn[:, h * 2048 + b * BANK:h * 2048 + (b + 1) * BANK],
                                            start=True, stop=True)
                last.then_inc(ready, 1)

            pe.wait_ge(maskn_ready, 1)
            for n in range(2 * HUB):
                hub_half(n, n // 2, n % 2, hubp, hub_used)
            pe.wait_ge(hub_done, 1)
            nc.tensor.transpose(ps[1][:, 0, 0:P], aggT, ident[:, :]).then_inc(hub_t, 1)
            pe.wait_ge(diffs, 1)
            nc.tensor.matmul(ps[1][0:1, 1, 0:2], ones[:, 0:1], ovd[:, :], start=True, stop=True).then_inc(flag_sum, 1)
            pe.wait_ge(flag_ready, 1)
            with pe.If(pe.value_load(flag[0:1, 0:1], min_val=0, max_val=1) > 0):
                with pe.Fori(0, NT) as t:
                    pe.wait_ge(gl0["mask"], t + 1)
                    pe.sem_inc(passed_pe, 1)
                    with pe.Fori(0, P) as i:
                        r = pe.snap(t * P + i)
                        for h in range(2):
                            hub_half(r * 2 + h, i, h, gl0["p"], gl0["used"])
                    pe.wait_ge(gl0["own"], (t + 1) * P)
                    nc.tensor.transpose(ps[0][:, 0, 0:P], aggT, ident[:, :]).then_inc(gl0["t"], 1)
                    pe.wait_ge(gl0["done"], t + 2)

            for b in range(8):
                pe.wait_ge(xn_ready, b + 1)
                for k in range(4):
                    last = nc.tensor.transpose(ps[0][:, 0, k * P:(k + 1) * P], xn[:, k, :], ident[:, :])
                last.then_inc(xnt, 1)
                pe.wait_ge(ht_ready, b + 1)
                if b:
                    pe.wait_ge(hr_ready, b)
                for k in range(4):
                    nc.tensor.matmul(ps[0][:, 1, k * F:(k + 1) * F], hTs[:, k * P:(k + 1) * P], Ws[:, :],
                                     start=True, stop=True)
                    last = nc.tensor.matmul(ps[0][:, 2, 2 * k:2 * k + 2], hTs[:, k * P:(k + 1) * P], Wa[:, :],
                                            start=True, stop=True)
                last.then_inc(h_mm, 1)

            def dense(sems, n):
                pe.wait_ge(sems["out"], n + 1)
                for h in range(2):
                    if h:
                        pe.wait_ge(sems["bc_act"], n * 2 + 1)
                        pe.wait_ge(sems["bc_dve"], n * 2 + 1)
                    for c in range(16):
                        t = 16 * h + c
                        for col, half in ((F, 0), (F + 1, 1)):
                            last = nc.tensor.matmul(ps[half][:, c // 4, c % 4 * P:(c % 4 + 1) * P],
                                                    HR[:, t, col:col + 1].to_broadcast([P, P]), ident[:, :],
                                                    start=True, stop=True)
                    last.then_inc(sems["bc"], 1)
                pe.wait_ge(sems["att"], n + 1)
                for b in range(9):
                    if b < 8:
                        if b >= 2:
                            pe.wait_ge(sems["copied"], n * 8 + (b - 1))
                        for k in range(4):
                            col = (4 * b + k) * P
                            last = nc.tensor.transpose(ps[0][:, b % 2, k * P:(k + 1) * P], T[:, col:col + P], ident[:, :])
                        last.then_inc(sems["turned"], 1)
                    if b >= 1:
                        c = b - 1
                        pe.wait_ge(sems["copied"], n * 8 + (c + 1))
                        for k in range(4):
                            last = nc.tensor.matmul(ps[1][:, 0, 0:F], attT[:, c % 2, k * P:(k + 1) * P],
                                                    HR[:, 4 * c + k, 0:F], start=(c == 0 and k == 0),
                                                    stop=(c == 7 and k == 3))
                        last.then_inc(sems["summed"], 1)

            pe.wait_ge(hr_ready, 8)
            dense(ds1, 0)
            with pe.If(pe.value_load(flag[0:1, 0:1], min_val=0, max_val=1) > 0):
                pe.wait_ge(ds1["out"], 2)
                pe.sem_inc(gl1["summed"], 1)
                with pe.Fori(0, NT) as t:
                    dense(gl1, t)

        @block.vector
        def _(v):
            own = [0]

            def inc(ins):
                ins.then_inc(dve, 1)
                own[0] += 1
                return own[0]

            def done(ins):
                v.wait_ge(dve, inc(ins))

            v.wait_ge(x_in, 16)
            for t in range(NT):
                inc(v.bn_stats(st6[:, t, :], xs[:, t, :]))
            v.wait_ge(dve, own[0])
            for t in range(NT):
                inc(v.bn_aggr(mv[:, t, :], st6[:, t, :]))
            v.wait_ge(dve, own[0])
            v.sem_inc(stats0, 1)
            v.wait_ge(sd0, 1)
            v.reciprocal(rstd[:, :], sd[:, :]).then_inc(rstd0, 1)
            v.wait_ge(consts, 1)
            for c in range(CPS):
                inc(v.tensor_scalar(diag[:, c, :], ident[:, :], kcol[:, c:c + 1], None, ALU.mult))
            inc(v.tensor_copy(identh[:, :], ident[:, :]))
            done(v.tensor_scalar(rowmask[:, :], rowmask[:, :], float(HUB), None, ALU.is_ge))
            v.sem_inc(consts2, 1)
            v.sem_inc(keys_used, 4)
            v.sem_inc(hub_used, 2)
            v.sem_inc(picked, 1)
            v.sem_inc(ds1["out"], 1)

            for seg in range(SEG):
                v.wait_ge(keys_ready, seg + 1)
                per = PIECES // SEG
                for q in range(per):
                    last = v.max(K0[:, (seg * per + q) * M8:(seg * per + q + 1) * M8],
                                 ps[0][:, seg % 4, q * (BANK // per):(q + 1) * (BANK // per)])
                last.then_inc(keys_used, 1)
            for seg in range(SEG):
                v.wait_ge(keys_ready, SEG + seg + 1)
                v.max(K[0][:, 1, seg * M8:(seg + 1) * M8], ps[0][:, seg % 4, :]).then_inc(keys_used, 1)

            def search(g, first, tiles):
                with v.Fori(0, tiles // 2) as i:
                    for k in range(2):
                        t = T0G[g] + first + k
                        v.wait_ge(picked, i * 2 + (t - 1))
                        for seg in range(SEG):
                            v.wait_ge(keys_ready, i * (2 * SEG) + (t * SEG + seg + 1))
                            v.sem_inc(passed_v, 1)
                            v.max(st[:, k, seg * M8:(seg + 1) * M8], ps[0][:, seg % 4, :]).then_inc(keys_used, 1)
                        v.wait_ge(keys_used, i * (2 * SEG) + (4 + (t + 1) * SEG))
                        v.tensor_copy(K[g][:, bass.ds(i * 2 + (first + k), 1), :].rearrange("p a m -> p (a m)"),
                                      st[:, k, :]).then_inc(picked, 1)
                v.wait_ge(picked, T0G[g] + first + tiles - 1)

            def queue(g):
                T, cap = TG[g], CAP[g]
                Kg, L = K[g], L3[g]
                first = 1 - g
                tmp = tmpk[:, 0:T * SEG * M8].rearrange("p (t s m) -> p t s m", s=SEG, m=M8)
                k4 = Kg[:, first:T, :].rearrange("p t (s m) -> p t s m", m=M8)
                done(v.tensor_reduce(ovs[:, g:g + 1], k4[:, :, :, M8 - 1], mybir.AxisListType.XY, ALU.max))
                if g == 0:
                    done(v.tensor_scalar(K0, K0, rowmask[:, 0:1], None, ALU.mult))
                    done(v.tensor_reduce(ovs[:, 2:3], K0.rearrange("p (q m) -> p q m", m=M8)[:, :, M8 - 1], X, ALU.max))
                    done(v.tensor_scalar(tmpk[:, 0:PIECES * M8], K0, 0.0, None, ALU.is_gt))
                    done(v.tensor_reduce(cnt[0][:, 0:1], tmpk[:, 0:PIECES * M8], X, ALU.add))
                    off = offs[:, :, None, :].to_broadcast([P, SEG, PIECES // SEG, M8])
                    t0v = tmpk[:, 0:PIECES * M8].rearrange("p (s q m) -> p s q m", s=SEG, m=M8)
                    done(v.tensor_tensor(t0v, t0v, off, ALU.mult))
                    done(v.tensor_tensor(K0, K0, tmpk[:, 0:PIECES * M8], ALU.add))
                    for r in range(LIST0 // M8):
                        done(v.max(L[:, r * M8:(r + 1) * M8], K0))
                        if r + 1 < LIST0 // M8:
                            done(v.match_replace(K0, L[:, r * M8:(r + 1) * M8], K0, 0.0))
                    inc(v.tensor_copy(ovs[:, 3:4], L[:, LIST0 - 1:LIST0]))
                tm = tmpk[:, first * SEG * M8:T * SEG * M8]
                kf = Kg[:, first:T, :].rearrange("p t m -> p (t m)")
                done(v.tensor_scalar(tm, kf, 0.0, None, ALU.is_gt))
                done(v.tensor_reduce(cnt[g][:, first:T], tm.rearrange("p (t m) -> p t m", m=SEG * M8), X, ALU.add))
                of = offs[:, :, :].rearrange("p s m -> p (s m)")[:, None, :].to_broadcast([P, T - first, SEG * M8])
                t3 = tm.rearrange("p (t m) -> p t m", m=SEG * M8)
                done(v.tensor_tensor(t3, t3, of, ALU.mult))
                done(v.tensor_tensor(kf, kf, tm, ALU.add))
                w0 = LIST0 if g == 0 else 0
                Lr = L[:, w0:].rearrange("p (t m) -> p t m", m=LIST[g])
                for r in range(LIST[g] // M8):
                    for t in range(first, T):
                        n = inc(v.max(Lr[:, t - first, r * M8:(r + 1) * M8], Kg[:, t, :]))
                    v.wait_ge(dve, n)
                    if r + 1 < LIST[g] // M8:
                        for t in range(first, T):
                            n = inc(v.match_replace(Kg[:, t, :], Lr[:, t - first, r * M8:(r + 1) * M8], Kg[:, t, :], 0.0))
                        v.wait_ge(dve, n)
                inc(v.tensor_reduce(ovs[:, 4 + g:5 + g], Lr[:, :, LIST[g] - 1], X, ALU.max))
                tl = tmpk[:, 0:L3W[g] - w0]
                done(v.tensor_scalar(tl, L[:, w0:], 0.0, float(N), ALU.is_gt, ALU.mult))
                tl3 = tl.rearrange("p (t m) -> p t m", m=LIST[g])
                done(v.tensor_tensor(tl3, tl3, tnum[:, first:T, None].to_broadcast([P, T - first, LIST[g]]), ALU.mult))
                done(v.tensor_tensor(L[:, w0:], L[:, w0:], tl, ALU.add))
                for r in range(cap // M8):
                    done(v.max(Q[g][:, r * M8:(r + 1) * M8], L[:, :]))
                    if r + 1 < cap // M8:
                        done(v.match_replace(L[:, :], Q[g][:, r * M8:(r + 1) * M8], L[:, :], 0.0))
                q_ = Q[g][:, :]
                inc(v.tensor_copy(ovs[:, 6 + g:7 + g], Q[g][:, cap - 1:cap]))
                inc(v.tensor_scalar(pad[:, 0:cap], q_, 0.5, float(2 * N), ALU.is_lt, ALU.mult))
                done(v.tensor_scalar(qi[:, 0:cap], q_, -1.0, None, ALU.add))
                done(v.tensor_scalar(idx[g][:, :], qi[:, 0:cap], N - 1, None, ALU.bitwise_and))
                v.tensor_tensor(idx[g][:, :], idx[g][:, :], pad[:, 0:cap], ALU.add).then_inc(queue_ready, 1)
                done(v.tensor_scalar(ti[:, 0:cap], qi[:, 0:cap], N.bit_length() - 1, None, ALU.arith_shift_right))
                done(v.tensor_copy(tf[g][:, :], ti[:, 0:cap]))
                inc(v.memset(cont[g][:, 0:1], 0.0))
                done(v.tensor_tensor(cont[g][:, 1:], tf[g][:, 1:], tf[g][:, 0:cap - 1], ALU.is_equal))
                done(v.tensor_tensor_scan(pre[:, 0:T], onesr[:, 0:T], cnt[g][:, :], 0.0, ALU.mult, ALU.add))
                done(v.tensor_tensor(ef[:, 0:T], cnt[g][:, :], pre[:, 0:T], ALU.subtract))
                done(v.tensor_scalar(ef[:, 0:T], ef[:, 0:T], pre[:, T - 1:T], None, ALU.add))
                if g == 0:
                    done(v.tensor_scalar(ovt[:, 0:1], ef[:, 1:2], float(CAP1[0]), None, ALU.is_gt))
                done(v.tensor_scalar(ef[:, 0:T], ef[:, 0:T], pcol[:, g:g + 1], None, ALU.add))
                done(v.tensor_scalar(pre[:, 0:T], cnt[g][:, :], 0.5, float(P * N), ALU.is_lt, ALU.mult))
                done(v.tensor_tensor(ef[:, 0:T], ef[:, 0:T], pre[:, 0:T], ALU.add))
                done(v.tensor_scalar(eidx[g][:, :], ef[:, 0:T], float(P * CAP[g]), None, ALU.min))
                c1 = CAP1[g]
                inc(v.memset(nend[g][:, c1 - 1:c1], 0.0))
                inc(v.tensor_copy(nend[g][:, 0:c1 - 1], cont[g][:, 1:c1]))
                inc(v.tensor_scalar(reset[g][:, :], cont[g][:, 0:c1], BIG, -BIG, ALU.mult, ALU.add))
                done(v.tensor_tensor_scan(nq[g][:, :], cont[g][:, 0:c1], onesr[:, 0:c1], 0.0, ALU.mult, ALU.add))
                spread(g, nq[g][:, :], nq[g][:, :], c1)

            def spread(g, out_, in_, c1):
                done(v.tensor_tensor(qe[:, 0:c1], in_, nend[g][:, :], ALU.mult))
                done(v.tensor_tensor(qe[:, 0:c1], in_, qe[:, 0:c1], ALU.subtract))
                done(v.tensor_tensor_scan(out_[:, ::-1], nend[g][:, ::-1], qe[:, 0:c1][:, ::-1], 0.0, ALU.mult, ALU.add))

            search(0, 2, TG[0] - 2)
            queue(0)
            search(1, 0, TG[1])
            queue(1)

            v.wait_ge(stage_used, NT + 1)
            inc(v.tensor_reduce(ovt[:, 1:2], ovs[:, :], X, ALU.max))
            inc(v.tensor_reduce(ovt[:, 2:3], sgn[:, :], X, ALU.add))
            for g in range(2):
                inc(v.tensor_reduce(ovt[:, 3 + g:4 + g], cnt[g][:, :], X, ALU.add))
            v.wait_ge(dve, own[0])
            done(v.tensor_scalar(ovt[:, 1:2], ovt[:, 1:2], 0.0, None, ALU.is_gt))
            inc(v.tensor_tensor(ovd[:, 0:1], ovt[:, 0:1], ovt[:, 1:2], ALU.add))
            done(v.tensor_tensor(ovt[:, 3:4], ovt[:, 3:4], ovt[:, 4:5], ALU.add))
            done(v.tensor_tensor(ovd[:, 1:2], ovt[:, 3:4], ovt[:, 2:3], ALU.subtract))
            v.sem_inc(diffs, 1)

            v.wait_ge(adjn_in, 16)
            v.tensor_scalar(maskn, adjn, 0.0, None, ALU.not_equal).then_inc(maskn_ready, 1)

            def hub_half(n, h, ready, used, to):
                v.wait_ge(ready, n + 1)
                v.wait_ge(used, n + 2)
                if not isinstance(n, int):
                    v.sem_inc(passed_v, 1)
                v.tensor_tensor_reduce(out=junk[:, 0:2048], in0=ps[h][:, :, :].rearrange("p b n -> p (b n)"),
                                       in1=HT[:, h * 2048:(h + 1) * 2048], scale=1.0,
                                       scalar=hm[:, 0:1] if h else 0.0, op0=ALU.mult, op1=ALU.max,
                                       accum_out=to if h else hm[:, 0:1]).then_inc(used, 1)

            v.wait_ge(h0t_used, 8)
            done(v.memset(aggT, 0.0))
            hubs = 0

            def accumulate(n, first):
                l, g, c = CHUNKS[n]
                v.wait_ge(gath[slot(n)], gathered(n))
                if n >= RSLOTS:
                    v.wait_ge(stored[n % RSLOTS], rstored(n - RSLOTS))
                for e in range(CH):
                    at = c * CH + e
                    new = R[:, n % RSLOTS, e, :]
                    old = R[:, (n if e else n - 1) % RSLOTS, (e - 1) % CH, :]
                    row = G[:, slot(n) * CH + e, 0:F]
                    if l:
                        k = sum(CAP1[:g]) + at
                        v.wait_ge(wg_ready, k + 1)
                        row = WG[:, k % 4, :]
                    if at == 0:
                        ins = v.tensor_copy(new, row)
                    else:
                        ins = v.scalar_tensor_tensor(new, old, cont[g][:, at:at + 1], row, ALU.mult,
                                                     ALU.add if l else ALU.max)
                    if l:
                        ins.then_inc(wg_used, 1)
                        v.wait_ge(wg_used, k + 1)
                    else:
                        done(ins)
                v.sem_inc(chunk_used, 1)

            for n in range(L0CH):
                accumulate(n, L0CH)
                for _ in range(2):
                    if hubs < 2 * HUB:
                        hub_half(hubs, hubs % 2, hubp, hub_used, aggT[:, hubs // 2:hubs // 2 + 1])
                        hubs += 1
            v.wait_ge(hub_used, 2 * HUB + 2)
            v.sem_inc(hub_done, 1)
            v.wait_ge(flag_sum, 1)
            done(v.tensor_scalar(flagf[:, :], ps[1][0:1, 1, 0:2], 0.0, None, ALU.not_equal))
            v.tensor_tensor(flag[:, :], flagf[:, 0:1], flagf[:, 1:2], ALU.max).then_inc(flag_ready, 1)
            v.wait_ge(hub_t, 1)
            v.wait_ge(ends[0][0], 16 * 4)
            done(v.tensor_copy(A[0:HUB, 0, :], ps[1][0:HUB, 0, 0:P]))

            v.wait_ge(flag_ready, 1)
            with v.If(v.value_load(flag[0:1, 0:1], min_val=0, max_val=1) > 0):
                for b in range(8):
                    v.wait_ge(ends[0][b], 16 * 4)
                v.sem_inc(gl0["used"], 2)
                v.sem_inc(gl0["done"], 1)
                with v.Fori(0, NT) as t:
                    v.wait_ge(gl0["in"], (t + 1) * 16)
                    v.tensor_scalar(maskn, adjn, 0.0, None, ALU.not_equal).then_inc(gl0["mask"], 1)
                    with v.Fori(0, P) as i:
                        r = v.snap(t * P + i)
                        for h in range(2):
                            hub_half(r * 2 + h, h, gl0["p"], gl0["used"], hm[:, 1:2])
                        v.wait_ge(gl0["used"], r * 2 + 4)
                        v.tensor_copy(aggT[:, bass.ds(i, 1)], hm[:, 1:2]).then_inc(gl0["own"], 1)
                        v.wait_ge(gl0["own"], r + 1)
                    v.wait_ge(gl0["t"], t + 1)
                    v.tensor_copy(A[:, bass.ds(t, 1), :].rearrange("p a f -> p (a f)"),
                                  ps[0][:, 0, 0:P]).then_inc(gl0["done"], 1)
                v.wait_ge(gl0["done"], NT + 1)

            def head(b):
                ts = slice(4 * b, 4 * b + 4)
                v.wait_ge(ends[0][b], 16 * 4)
                done(v.tensor_tensor(xs[:, ts, :], xs[:, ts, :], A[:, ts, :], ALU.add))
                for t in range(4 * b, 4 * b + 4):
                    inc(v.bn_stats(st6[:, t, :], xs[:, t, :]))
                v.wait_ge(dve, own[0])
                for t in range(4 * b, 4 * b + 4):
                    inc(v.bn_aggr(mv[:, t, :], st6[:, t, :]))
                v.wait_ge(dve, own[0])
                v.sem_inc(var1, 1)
                v.wait_ge(sd1, b + 1)
                done(v.reciprocal(rstd[:, ts], sd[:, ts]))
                if b:
                    v.wait_ge(xnt, b)
                for k in range(4):
                    t = 4 * b + k
                    inc(v.tensor_scalar(xn[:, k, :], xs[:, t, :], mv[:, t, 0:1], rstd[:, t:t + 1], ALU.subtract, ALU.mult))
                v.wait_ge(dve, own[0])
                v.sem_inc(xn_ready, 1)

            def tail(b):
                ts = slice(4 * b, 4 * b + 4)
                v.wait_ge(hr_copied, 4 * b + 4)
                sd_ = ps[0][:, 2, 0:8].rearrange("p (k c) -> p k c", c=2)
                inc(v.tensor_copy(S[:, ts], sd_[:, :, 0]))
                inc(v.tensor_copy(HR[:, ts, F], sd_[:, :, 1]))
                inc(v.tensor_scalar(HR[:, ts, F + 1], hsum[:, ts], 0.0, None, ALU.not_equal))
                done(v.memset(HR[:, ts, F + 2:ROW], 0.0))
                v.sem_inc(hr_ready, 1)

            for b in range(8):
                head(b)
                if b:
                    tail(b - 1)
            tail(7)

            def dense(sems, n, tile):
                steps = 14

                def mine(k, ins):
                    ins.then_inc(sems["own"], 1)
                    v.wait_ge(sems["own"], n * steps + k)

                v.tensor_copy(dn[:, 0:1], S[:, tile]).then_inc(sems["score"], 1)
                v.wait_ge(sems["in"], (n + 1) * 16)
                for h in range(2):
                    cols = slice(h * 2048, (h + 1) * 2048)
                    v.wait_ge(sems["bc"], n * 2 + (h + 1))
                    v.scalar_tensor_tensor(V[:, cols], adjn[:, cols], 0.0, ps[1][:, :, :].rearrange("p b n -> p (b n)"),
                                           ALU.is_gt, ALU.mult, accum_out=dn[:, 1 + h:2 + h]).then_inc(sems["bc_dve"], 1)
                v.wait_ge(sems["bc_dve"], n * 2 + 2)
                v.wait_ge(sems["bc_act"], n * 2 + 2)
                mine(1, v.tensor_tensor(dn[:, 5:6], dn[:, 1:2], dn[:, 2:3], ALU.add))
                mine(2, v.scalar_tensor_tensor(U, U, ALPHA, U, ALU.mult, ALU.max))
                mine(3, v.tensor_tensor(U, U, V, ALU.mult))
                mine(4, v.tensor_scalar(T, V, -NEG, NEG, ALU.mult, ALU.add))
                mine(5, v.tensor_tensor(U, U, T, ALU.add))
                mine(6, v.tensor_reduce(dn[:, 6:7], U, X, ALU.max))
                mine(7, v.tensor_scalar(dn[:, 3:4], dn[:, 6:7], -1.0, None, ALU.mult))
                v.sem_inc(sems["masked"], 1)
                v.wait_ge(sems["exp"], n + 1)
                mine(8, v.reciprocal(dn[:, 8:9], dn[:, 4:5]))
                mine(9, v.scalar_tensor_tensor(U, U, dn[:, 8:9], V, ALU.mult, ALU.mult))
                mine(10, v.tensor_reduce(dn[:, 6:7], U, X, ALU.max))
                mine(11, v.tensor_scalar(dn[:, 7:8], dn[:, 6:7], THR, None, ALU.is_gt))
                mine(12, v.tensor_tensor(dn[:, 7:8], dn[:, 7:8], dn[:, 5:6], ALU.mult))
                mine(13, v.scalar_tensor_tensor(T, U, THR, U, ALU.is_ge, ALU.mult))
                v.sem_inc(sems["att"], 1)
                v.wait_ge(sems["summed"], n * 8 + 9)
                mine(14, v.tensor_scalar(A[:, tile, :].rearrange("p a f -> p (a f)"), ps[1][:, 0, 0:F],
                                         dn[:, 7:8], None, ALU.mult))
                v.sem_inc(sems["out"], 1)

            dense(ds1, 0, slice(0, 1))

            for g in range(2):
                c1 = CAP1[g]
                done(v.memset(sq[g], 0.0))
                for t in range(1 - g, TG[g]):
                    tile = T0G[g] + t
                    done(v.tensor_scalar(qe[:, 0:c1], tf[g][:, 0:c1], float(t), S[:, tile:tile + 1], ALU.is_equal, ALU.mult))
                    done(v.tensor_tensor(sq[g], sq[g], qe[:, 0:c1], ALU.add))

            for g in range(2):
                c1 = CAP1[g]
                D, VV, m, ex, exn, z, top = (qv[:, k, 0:c1] for k in (0, 1, 3, 4, 5, 6, 7))
                u = qv[:, 2, 0:c1]
                for c in range(NCH1[g]):
                    n = FIRST[1, g] + c
                    v.wait_ge(gath[slot(n)], gathered(n))
                    inc(v.tensor_copy(qv[:, 0, c * CH:(c + 1) * CH], G[:, slot(n) * CH:(slot(n) + 1) * CH, F]))
                    inc(v.tensor_copy(qv[:, 1, c * CH:(c + 1) * CH], G[:, slot(n) * CH:(slot(n) + 1) * CH, F + 1]))
                v.wait_ge(dve, own[0])
                done(v.scalar_tensor_tensor(VV, tf[g][:, 0:c1], float(1 - g), VV, ALU.is_ge, ALU.mult))
                done(v.tensor_tensor(u, D, sq[g], ALU.add))
                done(v.scalar_tensor_tensor(u, u, ALPHA, u, ALU.mult, ALU.max))
                inc(v.tensor_tensor(u, u, VV, ALU.mult))
                done(v.tensor_scalar(z, VV, -NEG, NEG, ALU.mult, ALU.add))
                done(v.tensor_tensor(u, u, z, ALU.add))
                done(v.tensor_tensor_scan(m, reset[g][:, :], u, -BIG, ALU.add, ALU.max))
                spread(g, m, m, c1)
                done(v.tensor_scalar(m, m, NEG, None, ALU.max))
                inc(v.tensor_tensor(ex, u, m, ALU.subtract))
                done(v.tensor_scalar(exn, m, -1.0, NEG, ALU.mult, ALU.add))
                v.sem_inc(exq, 2)
                inc(v.tensor_scalar(D, nq[g][:, :], -1.0, float(N), ALU.mult, ALU.add))
                done(v.tensor_tensor_scan(top, cont[g][:, 0:c1], VV, 0.0, ALU.mult, ALU.add))
                spread(g, wq[g], top, c1)
                v.wait_ge(exq_done, g + 1)
                inc(v.tensor_tensor(D, D, exn, ALU.mult))
                done(v.tensor_tensor_scan(z, cont[g][:, 0:c1], ex, 0.0, ALU.mult, ALU.add))
                spread(g, z, z, c1)
                done(v.tensor_tensor(z, z, D, ALU.add))
                done(v.reciprocal(z, z))
                done(v.tensor_tensor(ex, ex, z, ALU.mult))
                done(v.tensor_tensor(ex, ex, VV, ALU.mult))
                done(v.tensor_tensor_scan(top, cont[g][:, 0:c1], ex, 0.0, ALU.mult, ALU.max))
                spread(g, top, top, c1)
                done(v.scalar_tensor_tensor(ex, ex, THR, ex, ALU.is_ge, ALU.mult))
                done(v.scalar_tensor_tensor(ex, top, THR, ex, ALU.is_gt, ALU.mult))
                done(v.tensor_tensor(wq[g], wq[g], ex, ALU.mult))
                v.sem_inc(w_ready, 1)
                for n in range(FIRST[1, g], FIRST[1, g] + NCH1[g]):
                    accumulate(n, 0)

            for b in range(8):
                v.wait_ge(ends[1][b], 16 * (3 if b == 0 else 4))
            with v.If(v.value_load(flag[0:1, 0:1], min_val=0, max_val=1) > 0):
                v.sem_inc(gl1["out"], 1)
                with v.Fori(0, NT) as t:
                    dense(gl1, t, bass.ds(t, 1))

            def elu_head(b):
                ts = slice(4 * b, 4 * b + 4)
                done(v.tensor_tensor(zv[b % 2], HR[:, ts, 0:F], A[:, ts, :], ALU.add))
                done(v.tensor_scalar(ezv[b % 2], zv[b % 2], 0.0, None, ALU.min))
                v.sem_inc(z_ready, 1)

            def elu_tail(b):
                ts = slice(4 * b, 4 * b + 4)
                v.wait_ge(ez_ready, b + 1)
                done(v.scalar_tensor_tensor(zv[b % 2], zv[b % 2], 0.0, ezv[b % 2], ALU.max, ALU.add))
                done(v.scalar_tensor_tensor(xs[:, ts, :], zv[b % 2], -1.0, xs[:, ts, :], ALU.add, ALU.add))
                v.sem_inc(o_ready, 1)

            for b in range(8):
                elu_head(b)
                if b:
                    elu_tail(b - 1)
            elu_tail(7)


def kernel(x, adj, L1_gnn_W, L1_gnn_a):
    import numpy as np
    from concourse import bacc
    from concourse.bass_utils import run_bass_kernel_spmd

    x, adj, w, a = (np.ascontiguousarray(v) for v in (x, adj, L1_gnn_W, L1_gnn_a))
    adj_t = np.ascontiguousarray(adj.reshape(NT, P, CPS, P, SEG).transpose(0, 3, 4, 2, 1)).reshape(NT * P, N)
    a = np.ascontiguousarray(a.reshape(2, F).T)
    nc = bacc.Bacc("TRN2", target_bir_lowering=False, num_devices=1)
    arrays, args = {}, []
    for name, v in (("x", x), ("adj", adj), ("adj_t", adj_t), ("w", w), ("a", a)):
        arrays[f"in_{name}"] = v
        args.append(nc.dram_tensor(f"in_{name}", v.shape, mybir.dt.from_np(v.dtype), kind="ExternalInput").ap())
    args.append(nc.dram_tensor("out", (N, F), f32, kind="ExternalOutput").ap())
    build(nc, *args)
    return run_bass_kernel_spmd(nc, [arrays], core_ids=[0]).results[0]["out"]
```

```python
from contextlib import ExitStack

import concourse.bass as bass
from concourse import mybir

N, F, P = 4096, 128, 128
NT = N // P
SEG = 8
CPS = N // SEG // P
M8 = 8
HUB = 12
PIECES = 64
GROUPS = 3
T0G = (0, 4, 16)
TG = (4, 12, 16)
CAP = (80, 72, 64)
CAP1 = (48, 72, 64)
ORDER = ((0, 1, 2), (1, 2, 0))
LIST = (32, 24, 16)
LIST0 = 56
BOTH = 16
TILE = 1 << 14
CH = 8
BEHIND = 12
TURNS = 6
SLOTS = 13
RSLOTS = 4
ROW = 132
STAGES = 3
BANK = 512
EARLY = 8
BANKS = 4
EPS, ALPHA, THR, NEG, BIG = 1e-5, 0.2, 1e-4, -1e9, 3e38

DENSE = ("in", "score", "bc", "bc_act", "bc_dve", "masked", "exp", "att", "turned", "copied", "summed", "own", "out")

f32, f16, bf16, i32 = mybir.dt.float32, mybir.dt.float16, mybir.dt.bfloat16, mybir.dt.int32
ALU = mybir.AluOpType
ACT = mybir.ActivationFunctionType
X = mybir.AxisListType.X


def build(nc, x, adj, adj_t, w, a, out):
    t0 = nc.dram_tensor("h0_rows", [N, F], f32, kind="Internal").ap()
    t1 = nc.dram_tensor("h_rows", [N, ROW], f32, kind="Internal").ap()
    run = [nc.dram_tensor(f"running{g}", [P * CAP[g] + 1, F], f32, kind="Internal").ap() for g in range(GROUPS)]

    ctx = ExitStack()
    with ctx:
        def sb(name, shape, dt=f32):
            return ctx.enter_context(nc.sbuf_tensor(name, shape, dt))

        def sem(name):
            return ctx.enter_context(nc.semaphore(name))

        xs = sb("xs", [P, NT, F])
        G = sb("gathered", [P, SLOTS * CH, ROW])
        R = sb("running", [P, RSLOTS, CH, F])
        h0 = R[:, :, :, :].rearrange("p s e f -> p (s e) f")
        HB = sb("h_store", [P, NT * ROW])
        HT = HB[:, 0:N]
        HR = HB[:, :].rearrange("p (t c) -> p t c", c=ROW)
        arena = sb("arena", [P, 18432])
        stage = [arena[:, s * N:(s + 1) * N].bitcast(i32) for s in range(STAGES)]
        mask = [arena[:, 3 * N + s * N // 2:3 * N + (s + 1) * N // 2].bitcast(f16) for s in range(STAGES)]
        adjn = arena[:, 0:N].bitcast(i32)
        maskn = arena[:, N:N + N // 2].bitcast(f16)
        junk = arena[:, N + N // 2:2 * N]
        V = arena[:, 0:N]
        U = arena[:, N:2 * N]
        T = arena[:, 2 * N:3 * N]
        A = arena[:, 3 * N:4 * N].rearrange("p (t f) -> p t f", f=F)
        work = sb("work", [P, 2 * BANK + 8 * F])
        attT = work[:, 0:2 * BANK].rearrange("p (b n) -> p b n", b=2)
        xn = work[:, 2 * BANK:2 * BANK + 4 * F].rearrange("p (k f) -> p k f", f=F)
        hTs = work[:, 2 * BANK + 4 * F:2 * BANK + 8 * F]
        ident = sb("ident", [P, P])
        identh = sb("identh", [P, P], f16)
        diag = sb("diag", [P, CPS, P], f16)
        kcol = sb("kcol", [P, CPS])
        ones = sb("ones", [P, 1])
        rowmask = sb("rowmask", [P, 1])
        pcol = sb("pcol", [P, GROUPS])
        offs = sb("offs", [P, SEG, M8])
        tnum = sb("tnum", [P, max(TG)])
        qv = sb("qv", [P, 8, max(CAP1)])
        K0 = qv[:, :, :].rearrange("p a b -> p (a b)")[:, 0:PIECES * M8]
        K = sb("K", [P, 2, SEG * M8])
        LS = [LIST0 if g == 0 else 0 for g in range(GROUPS)]
        TL = [TG[g] - (g == 0) for g in range(GROUPS)]
        LW = [LS[g] + TL[g] * LIST[g] for g in range(GROUPS)]
        L = sb("L", [P, max(LW) + BOTH])
        LB = max(LW)
        li = sb("li", [P, LB], i32)
        lw = sb("lw", [P, LB], i32)
        lf = sb("lf", [P, LB])
        lh = sb("lh", [P, LB])
        lsec = sb("lsec", [P, LB])
        cnt = [sb(f"cnt{g}", [P, TG[g]]) for g in range(GROUPS)]
        pre = sb("pre", [P, max(TG)])
        Q = sb("Q", [P, max(CAP)])
        qi = sb("qi", [P, max(CAP)], i32)
        qn = sb("qn", [P, max(CAP)], i32)
        qb = sb("qb", [P, max(CAP)], i32)
        pad = sb("pad", [P, max(CAP)], i32)
        idx = [sb(f"idx{g}", [P, CAP[g]], i32) for g in range(GROUPS)]
        tf = [sb(f"tf{g}", [P, CAP[g]]) for g in range(GROUPS)]
        cont = [sb(f"cont{g}", [P, CAP[g]]) for g in range(GROUPS)]
        ef = sb("ef", [P, max(TG)])
        eidx = [sb(f"eidx{g}", [P, TG[g]], i32) for g in range(GROUPS)]
        nend = [sb(f"nend{g}", [P, CAP1[g]]) for g in range(GROUPS)]
        reset = [sb(f"reset{g}", [P, CAP1[g]]) for g in range(GROUPS)]
        nq = [sb(f"nq{g}", [P, CAP1[g]]) for g in range(GROUPS)]
        sgn = sb("sgn", [P, NT])
        ovs = sb("ovs", [P, NT + 3 * GROUPS + 1])
        ovd = sb("ovd", [P, 2])
        flagf = sb("flagf", [1, 2])
        flag = sb("flag", [1, 1], i32)
        st6 = sb("st6", [P, NT, 6])
        mv = sb("mv", [P, NT, 2])
        sd = sb("sd", [P, NT])
        rstd = sb("rstd", [P, NT])
        epsb = sb("epsb", [P, 1])
        hm = sb("hm", [P, 4])
        Ws = sb("Ws", [P, F])
        WT = sb("WT", [P, F])
        a2 = sb("a2", [P, 2])
        Wa = sb("Wa", [P, 2])
        S = sb("S", [P, NT])
        hsum = sb("hsum", [P, NT])
        tail_ = arena[:, 4 * N:]
        WG = tail_[:, 0:4 * F].rearrange("p (k f) -> p k f", f=F)
        aggT = tail_[:, 4 * F:4 * F + P]
        sq = [tail_[:, 5 * F + g * P:5 * F + g * P + CAP1[g]] for g in range(GROUPS)]
        wq = [tail_[:, 8 * F + g * P:8 * F + g * P + CAP1[g]] for g in range(GROUPS)]
        dn = sb("dn", [P, 12])
        zrow = sb("zrow", [1, F])
        onesr = sb("onesr", [P, max(CAP1)])
        qe = sb("qe", [P, max(CAP)])
        ovt = sb("ovt", [P, 4 + GROUPS])
        Z, EZ, O = (v_.rearrange("p (t f) -> p t f", f=F) for v_ in (U, T, V))

        ps = [ctx.enter_context(nc.psum_tensor(f"ps{b}", [P, 4, BANK], f32)) for b in range(2)]

        x_in = sem("x_in"); w_in = sem("w_in")
        adj_in = [sem(f"adj_in{s}") for s in range(STAGES)]
        stage_used = sem("stage_used")
        mask_used = sem("mask_used")
        keys_ready = sem("keys_ready")
        keys_used = sem("keys_used")
        last_mask = sem("last_mask")
        consts = sem("consts"); consts2 = sem("consts2")
        dve = sem("dve")
        pool = sem("pool")
        stats0 = sem("stats0"); centred = sem("centred"); sd0 = sem("sd0"); rstd0 = sem("rstd0"); h0_ready = sem("h0_ready")
        t0_in = sem("t0_in")
        h0t_ready = sem("h0t_ready"); h0t_used = sem("h0t_used")
        queue_ready = sem("queue_ready")
        gath = [sem(f"gath{s}") for s in range(SLOTS)]
        chunk_used = sem("chunk_used")
        stored = [sem(f"stored{s}") for s in range(RSLOTS)]
        zrow_in = sem("zrow_in")
        ends = [[sem(f"ends{l}_{b}") for b in range(8)] for l in range(2)]
        adjn_in = sem("adjn_in"); maskn_ready = sem("maskn_ready")
        hubp = sem("hubp"); hub_used = sem("hub_used"); hub_done = sem("hub_done"); hub_t = sem("hub_t")
        flag_sum = sem("flag_sum"); flag_ready = sem("flag_ready"); diffs = sem("diffs")
        wprep = sem("wprep"); wprep_c = sem("wprep_c")
        var1 = sem("var1"); sd1 = sem("sd1"); xn_ready = sem("xn_ready"); xnt = sem("xnt"); ht_ready = sem("ht_ready")
        h_mm = sem("h_mm"); hr_copied = sem("hr_copied"); hr_ready = sem("hr_ready")
        t1_in = sem("t1_in")
        exq = sem("exq"); exq_done = sem("exq_done"); w_ready = sem("w_ready")
        wg_ready = sem("wg_ready"); wg_used = sem("wg_used")
        ds1 = {n: sem(f"d_{n}") for n in DENSE}
        gl0 = {n: sem(f"g0_{n}") for n in ("in", "mask", "p", "used", "own", "t", "done")}
        gl1 = {n: sem(f"g1_{n}") for n in DENSE}
        elu = {n: sem(f"elu_{n}") for n in ("z", "ez", "o", "in")}
        gelu = {n: sem(f"gelu_{n}") for n in ("z", "ez", "o", "in")}

        passed_v = sem("passed_v"); passed_pe = sem("passed_pe")

        block = ctx.enter_context(nc.Block())

        adjt_v = adj_t.rearrange("(t p) n -> t p n", p=P)
        adj_v = adj.rearrange("(t p) n -> t p n", p=P)
        x_v = x.rearrange("(t p) f -> p t f", p=P)
        out_v = out.rearrange("(t p) f -> p t f", p=P)
        t0_v = t0.rearrange("(t p) f -> p t f", p=P)
        t1_v = t1.rearrange("(t p) c -> p t c", p=P)

        NCH = [[CAP[g] // CH for g in range(GROUPS)], [CAP1[g] // CH for g in range(GROUPS)]]
        CHUNKS = [(l, g, c) for l in range(2) for g in ORDER[l] for c in range(NCH[l][g])]
        FIRST = {(l, g): CHUNKS.index((l, g, 0)) for l in range(2) for g in range(GROUPS)}
        L0CH = sum(NCH[0])
        ELU = [b for g in ORDER[1] for b in range(T0G[g] // 4, (T0G[g] + TG[g]) // 4)]
        K1ST = {g: (FIRST[1, g] - L0CH) * CH for g in range(GROUPS)}
        BATCHES = [[b for b in range(8) if T0G[g] <= 4 * b < T0G[g] + TG[g]] for g in range(GROUPS)]

        def slot(n):
            return n % SLOTS

        def gathered(n):
            return 16 * CH * (n // SLOTS + 1)

        def rstored(n):
            return 16 * (n // RSLOTS + 1)

        LOOP = NT - 2

        @block.sync
        def _(sp):
            sp.dma_start(xs[:, :, :], x_v).then_inc(x_in, 16)
            for t in range(2):
                sp.dma_start(stage[t], adjt_v[t]).then_inc(adj_in[t], 16)
            sp.dma_start(Ws[:, :], w).then_inc(w_in, 16)
            sp.dma_start(a2[:, :], a).then_inc(w_in, 16)
            with sp.Fori(0, (NT - 2 - TURNS) // STAGES) as i:
                for k in range(STAGES):
                    s = (2 + k) % STAGES
                    sp.wait_ge(stage_used, i * STAGES + (k + 1))
                    sp.dma_start(stage[s], adjt_v[i * STAGES + (2 + k)]).then_inc(adj_in[s], 16)

            def store_chunk(n):
                l, g, c = CHUNKS[n]
                sp.wait_ge(chunk_used, n + 1)
                dst = run[g][0:P * CAP[g], :].rearrange("(p q) f -> p q f", p=P)
                sp.dma_start(dst[:, c * CH:(c + 1) * CH, :], R[:, n % RSLOTS, :, :]).then_inc(stored[n % RSLOTS], 16)

            for n in range(TURNS):
                t = NT - TURNS + n
                sp.wait_ge(stage_used, t - 1)
                sp.dma_start(stage[t % STAGES], adjt_v[t]).then_inc(adj_in[t % STAGES], 16)
                store_chunk(n)
            for n in range(TURNS, BEHIND):
                store_chunk(n)
            sp.wait_ge(stage_used, NT + 1)
            sp.wait_ge(mask_used, NT + 1)
            sp.dma_start(adjn, adj_v[0]).then_inc(adjn_in, 16)
            sp.wait_ge(consts2, 1)
            for g in range(GROUPS):
                sp.dma_start(run[g][P * CAP[g]:P * CAP[g] + 1, :], zrow[:, :]).then_inc(zrow_in, 16)

            for n in range(BEHIND, L0CH):
                store_chunk(n)
            sp.wait_ge(flag_ready, 1)
            with sp.If(sp.value_load(flag[0:1, 0:1], min_val=0, max_val=1) > 0):
                with sp.Fori(0, NT) as t:
                    sp.wait_ge(gl0["done"], t + 1)
                    sp.dma_start(adjn, adj_v[t]).then_inc(gl0["in"], 16)
                sp.wait_ge(gl0["done"], NT + 1)
            for b in range(8):
                sp.wait_ge(hr_ready, b + 1)
                sp.dma_start(t1_v[:, 4 * b:4 * b + 4, :], HR[:, 4 * b:4 * b + 4, :]).then_inc(t1_in, 16)
            sp.dma_start(adjn, adj_v[0]).then_inc(ds1["in"], 16)
            for n in range(L0CH, len(CHUNKS)):
                store_chunk(n)
            def store_out(sems, order):
                for n, b in enumerate(order):
                    sp.wait_ge(sems["o"], n + 1)
                    sp.dma_start(out_v[:, 4 * b:4 * b + 4, :], O[:, 4 * b:4 * b + 4, :]).then_inc(sems["in"], 16)
                sp.wait_ge(sems["in"], 16 * 8)

            store_out(elu, ELU)
            with sp.If(sp.value_load(flag[0:1, 0:1], min_val=0, max_val=1) > 0):
                with sp.Fori(0, NT) as t:
                    sp.wait_ge(gl1["out"], t + 1)
                    sp.dma_start(adjn, adj_v[t]).then_inc(gl1["in"], 16)
                store_out(gelu, range(8))

        @block.gpsimd
        def _(gp):
            own = [0]

            def step(ins):
                ins.then_inc(pool, 1)
                own[0] += 1
                return own[0]

            step(gp.memset(ident[:, :], 0.0))
            step(gp.iota(kcol[:, :], [[8, 2], [32 * P, 2]], base=8, channel_multiplier=32, allow_small_or_imprecise_dtypes=True))
            step(gp.iota(rowmask[:, :], [[0, 1]], base=0, channel_multiplier=1, allow_small_or_imprecise_dtypes=True))
            for g in range(GROUPS):
                step(gp.iota(pcol[:, g:g + 1], [[0, 1]], base=-1, channel_multiplier=CAP[g],
                             allow_small_or_imprecise_dtypes=True))
            step(gp.iota(offs[:, :, :], [[1, SEG], [0, M8]], base=0, channel_multiplier=0,
                         allow_small_or_imprecise_dtypes=True))
            step(gp.iota(tnum[:, :], [[1, max(TG)]], base=0, channel_multiplier=0, allow_small_or_imprecise_dtypes=True))
            step(gp.memset(ones[:, :], 1.0))
            step(gp.memset(onesr[:, :], 1.0))
            step(gp.memset(epsb[:, :], EPS))
            step(gp.memset(zrow[:, :], 0.0))
            n = own[0]
            gp.wait_ge(pool, n)
            step(gp.affine_select(out=ident[:, :], in_=ident[:, :], compare_op=ALU.not_equal, fill=1.0, base=0,
                                  pattern=[[-1, P]], channel_multiplier=1))
            n = step(gp.memset(G[:, :, :], 0.0))
            gp.wait_ge(pool, n)
            gp.sem_inc(consts, 1)
            gp.wait_ge(stats0, 1)
            mean = mv[:, :, 0:1].to_broadcast([P, NT, F])
            gp.tensor_tensor(h0, xs[:, :, :], mean, ALU.subtract).then_inc(centred, 1)
            gp.wait_ge(t0_in, 16)

            def gather_chunk(n):
                l, g, c = CHUNKS[n]
                if c == 0 and l == 0:
                    gp.wait_ge(queue_ready, ORDER[0].index(g) + 1)
                if n >= SLOTS:
                    gp.wait_ge(chunk_used, n - SLOTS + 1)
                for e in range(CH):
                    src, wide = (t0, F) if l == 0 else (t1, ROW)
                    gp.indirect_dma_start(
                        G[:, slot(n) * CH + e, 0:wide], None, src,
                        bass.IndirectOffsetOnAxis(ap=idx[g][:, c * CH + e:c * CH + e + 1], axis=0),
                        bounds_check=N - 1, oob_is_err=False).then_inc(gath[slot(n)], 16)

            def gather_ends(l, g):
                last = FIRST[l, g] + NCH[l][g] - 1
                for n in range(last - RSLOTS + 1, last + 1):
                    gp.wait_ge(stored[n % RSLOTS], rstored(n))
                for t in range(TG[g]):
                    if l == 1 and g == 0 and t == 0:
                        continue
                    tile = T0G[g] + t
                    gp.indirect_dma_start(
                        A[:, tile, :], None, run[g],
                        bass.IndirectOffsetOnAxis(ap=eidx[g][:, t:t + 1], axis=0),
                        bounds_check=P * CAP[g], oob_is_err=False).then_inc(ends[l][tile // 4], 16)

            for l in range(2):
                if l:
                    gp.wait_ge(t1_in, 16 * 8)
                first, second, third = ORDER[l]
                for g in (first, second):
                    for c in range(NCH[l][g]):
                        gather_chunk(FIRST[l, g] + c)
                if l == 0:
                    gp.wait_ge(zrow_in, 16 * GROUPS)
                    gp.wait_ge(last_mask, 1)
                gather_ends(l, first)
                for c in range(NCH[l][third]):
                    gather_chunk(FIRST[l, third] + c)
                gather_ends(l, second)
                gather_ends(l, third)

        @block.scalar
        def _(act):
            act.wait_ge(consts, 1)
            act.wait_ge(stats0, 1)
            nc.scalar.activation(sd[:, :], mv[:, :, 1], ACT.Sqrt, bias=epsb[:, 0:1]).then_inc(sd0, 1)
            act.wait_ge(wprep, 1)
            nc.scalar.activation(WT[:, :], ps[1][:, 3, 0:P], ACT.Copy).then_inc(wprep_c, 1)
            act.wait_ge(wprep, 2)
            nc.scalar.activation(Wa[:, :], ps[1][:, 2, 0:2], ACT.Copy).then_inc(wprep_c, 1)

            act.sem_inc(stage_used, 1)
            for t in range(2):
                act.wait_ge(adj_in[t], 16)
                src = stage[t].rearrange("p (c i) -> p c i", i=P)
                dst = mask[t].rearrange("p (c i) -> p c i", i=P)
                if t == 0:
                    nc.scalar.activation(dst[:, :, 0:HUB], src[:, :, 0:HUB], ACT.Sign)
                    nc.scalar.activation(dst[:, :, HUB:P], src[:, :, HUB:P], ACT.Sign,
                                         accum_out=sgn[:, 0:1]).then_inc(stage_used, 1)
                else:
                    nc.scalar.activation(dst, src, ACT.Sign, accum_out=sgn[:, t:t + 1]).then_inc(stage_used, 1)
            act.wait_ge(rstd0, 1)
            act.wait_ge(centred, 1)
            for t in range(NT):
                nc.scalar.activation(h0[:, t, :], h0[:, t, :], ACT.Relu, scale=rstd[:, t:t + 1]).then_inc(h0_ready, 1)
            act.wait_ge(h0_ready, NT)
            act.dma_start(t0_v, h0).then_inc(t0_in, 16)

            def signs(first, tiles):
                done = first - 2
                with act.Fori(0, tiles // STAGES) as i:
                    for k in range(STAGES):
                        s = (2 + k) % STAGES
                        act.wait_ge(adj_in[s], i * 16 + (done // STAGES * 16 + (16 if s == 2 else 32)))
                        act.wait_ge(mask_used, i * STAGES + (done + k + 1))
                        nc.scalar.activation(mask[s], stage[s], ACT.Sign,
                                             accum_out=sgn[:, bass.ds(i * STAGES + (first + k), 1)]).then_inc(stage_used, 1)

            signs(2, EARLY - 2)
            for b in range(8):
                act.wait_ge(h0t_ready, b + 1)
                nc.scalar.activation(HT[:, b * BANK:(b + 1) * BANK], ps[1][:, b % 4, :], ACT.Copy).then_inc(h0t_used, 1)
            signs(EARLY, NT - EARLY)

            for b in range(8):
                act.wait_ge(var1, b + 1)
                nc.scalar.activation(sd[:, 4 * b:4 * b + 4], mv[:, 4 * b:4 * b + 4, 1], ACT.Sqrt,
                                     bias=epsb[:, 0:1]).then_inc(sd1, 1)
                act.wait_ge(xnt, b + 1)
                nc.scalar.activation(hTs, ps[0][:, 0, :], ACT.Relu).then_inc(ht_ready, 1)
                act.wait_ge(h_mm, b + 1)
                for k in range(4):
                    t = 4 * b + k
                    nc.scalar.activation(HR[:, t, 0:F], ps[0][:, 1, k * F:(k + 1) * F], ACT.Copy,
                                         accum_out=hsum[:, t:t + 1]).then_inc(hr_copied, 1)

            def dense(sems, n):
                act.wait_ge(sems["score"], n + 1)
                for h in range(2):
                    act.wait_ge(sems["bc"], n * 2 + (h + 1))
                    nc.scalar.activation(U[:, h * 2048:(h + 1) * 2048], ps[0][:, :, :].rearrange("p b n -> p (b n)"),
                                         ACT.Identity, bias=dn[:, 0:1]).then_inc(sems["bc_act"], 1)
                act.wait_ge(sems["masked"], n + 1)
                nc.scalar.activation(U, U, ACT.Exp, bias=dn[:, 3:4], accum_out=dn[:, 4:5]).then_inc(sems["exp"], 1)
                for b in range(8):
                    act.wait_ge(sems["turned"], n * 8 + (b + 1))
                    act.wait_ge(sems["summed"], n * 8 + max(b, 1))
                    nc.scalar.activation(attT[:, b % 2, :], ps[0][:, b % 2, :], ACT.Copy).then_inc(sems["copied"], 1)

            def weigh(g):
                nth = ORDER[1].index(g)
                act.wait_ge(exq, nth + 1)
                c1 = CAP1[g]
                nc.scalar.activation(qv[:, 4, 0:c1], qv[:, 4, 0:c1], ACT.Exp)
                nc.scalar.activation(qv[:, 5, 0:c1], qv[:, 5, 0:c1], ACT.Exp).then_inc(exq_done, 1)
                act.wait_ge(w_ready, nth + 1)
                for e in range(c1):
                    k = K1ST[g] + e
                    if k >= 4:
                        act.wait_ge(wg_used, k - 3)
                    n = FIRST[1, g] + e // CH
                    nc.scalar.activation(WG[:, k % 4, :], G[:, slot(n) * CH + e % CH, 0:F], ACT.Copy,
                                         scale=wq[g][:, e:e + 1]).then_inc(wg_ready, 1)

            def exps(sems, first, n):
                for m in range(first, first + n):
                    b = ELU[m] if sems is elu else m
                    act.wait_ge(sems["z"], m + 1)
                    nc.scalar.activation(EZ[:, 4 * b:4 * b + 4, :], EZ[:, 4 * b:4 * b + 4, :], ACT.Exp).then_inc(sems["ez"], 1)

            dense(ds1, 0)
            done = 0
            for nth, g in enumerate(ORDER[1]):
                if nth == 2:
                    exps(elu, 0, len(BATCHES[ORDER[1][0]]))
                    done = len(BATCHES[ORDER[1][0]])
                weigh(g)
            exps(elu, done, 8 - done)
            act.wait_ge(flag_ready, 1)
            with act.If(act.value_load(flag[0:1, 0:1], min_val=0, max_val=1) > 0):
                with act.Fori(0, NT) as t:
                    dense(gl1, t)
                exps(gelu, 0, 8)

        @block.tensor
        def _(pe):
            pe.wait_ge(w_in, 32)
            pe.wait_ge(consts, 1)
            nc.tensor.transpose(ps[1][:, 3, 0:P], Ws[:, :], ident[:, :]).then_inc(wprep, 1)
            pe.wait_ge(wprep_c, 1)
            nc.tensor.matmul(ps[1][:, 2, 0:2], WT[:, :], a2[:, :], start=True, stop=True).then_inc(wprep, 1)
            pe.wait_ge(consts2, 1)

            pe.sem_inc(mask_used, 1)
            pe.sem_inc(ds1["summed"], 1)

            def keys(n, s):
                for bank in range(BANKS):
                    pe.wait_ge(keys_used, n + (bank + 1))
                    for piece in range(2):
                        for c in (0, 2, 1, 3):
                            col = ((2 * bank + piece) * CPS + c) * P
                            at = piece * 2 * P + c % 2 * P
                            last = nc.tensor.matmul(ps[0][:, bank, at:at + P], mask[s][:, col:col + P],
                                                    diag[:, c, :], start=c < 2, stop=c >= 2)
                    last.then_inc(keys_ready, 1)
                pe.wait_ge(keys_ready, n + BANKS)
                pe.sem_inc(mask_used, 1)

            def tiles(first, count):
                with pe.Fori(0, count // STAGES) as i:
                    for k in range(STAGES):
                        pe.wait_ge(stage_used, i * STAGES + (first + k + 2))
                        keys(i * (STAGES * BANKS) + (first + k) * BANKS, (2 + k) % STAGES)

            for t in range(2):
                pe.wait_ge(stage_used, t + 2)
                keys(t * BANKS, t)
            tiles(2, EARLY - 2)
            pe.wait_ge(h0_ready, NT)
            for b in range(8):
                if b >= 4:
                    pe.wait_ge(h0t_used, b - 3)
                for k in range(4):
                    last = nc.tensor.transpose(ps[1][:, b % 4, k * P:(k + 1) * P], h0[:, 4 * b + k, :], ident[:, :])
                last.then_inc(h0t_ready, 1)
            tiles(EARLY, NT - EARLY)
            pe.sem_inc(last_mask, 1)
            pe.wait_ge(h0t_used, 8)

            def hub_half(n, i, h, ready, used):
                pe.wait_ge(used, n + 1)
                row = identh[:, bass.ds(i, 1)].to_broadcast([P, P])
                for b in range(4):
                    last = nc.tensor.matmul(ps[h][:, b, :], row, maskn[:, h * 2048 + b * BANK:h * 2048 + (b + 1) * BANK],
                                            start=True, stop=True)
                last.then_inc(ready, 1)

            pe.wait_ge(maskn_ready, 1)
            for n in range(2 * HUB):
                hub_half(n, n // 2, n % 2, hubp, hub_used)
            pe.wait_ge(hub_done, 1)
            nc.tensor.transpose(ps[1][:, 0, 0:P], aggT, ident[:, :]).then_inc(hub_t, 1)
            pe.wait_ge(diffs, 1)
            nc.tensor.matmul(ps[1][0:1, 1, 0:2], ones[:, 0:1], ovd[:, :], start=True, stop=True).then_inc(flag_sum, 1)
            pe.wait_ge(flag_ready, 1)
            with pe.If(pe.value_load(flag[0:1, 0:1], min_val=0, max_val=1) > 0):
                with pe.Fori(0, NT) as t:
                    pe.wait_ge(gl0["mask"], t + 1)
                    pe.sem_inc(passed_pe, 1)
                    with pe.Fori(0, P) as i:
                        r = pe.snap(t * P + i)
                        for h in range(2):
                            hub_half(r * 2 + h, i, h, gl0["p"], gl0["used"])
                    pe.wait_ge(gl0["own"], (t + 1) * P)
                    nc.tensor.transpose(ps[0][:, 0, 0:P], aggT, ident[:, :]).then_inc(gl0["t"], 1)
                    pe.wait_ge(gl0["done"], t + 2)

            for b in range(8):
                pe.wait_ge(xn_ready, b + 1)
                for k in range(4):
                    last = nc.tensor.transpose(ps[0][:, 0, k * P:(k + 1) * P], xn[:, k, :], ident[:, :])
                last.then_inc(xnt, 1)
                pe.wait_ge(ht_ready, b + 1)
                if b:
                    pe.wait_ge(hr_ready, b)
                for k in range(4):
                    nc.tensor.matmul(ps[0][:, 1, k * F:(k + 1) * F], hTs[:, k * P:(k + 1) * P], Ws[:, :],
                                     start=True, stop=True)
                    last = nc.tensor.matmul(ps[0][:, 2, 2 * k:2 * k + 2], hTs[:, k * P:(k + 1) * P], Wa[:, :],
                                            start=True, stop=True)
                last.then_inc(h_mm, 1)

            def dense(sems, n):
                pe.wait_ge(sems["out"], n + 1)
                for h in range(2):
                    if h:
                        pe.wait_ge(sems["bc_act"], n * 2 + 1)
                        pe.wait_ge(sems["bc_dve"], n * 2 + 1)
                    for c in range(16):
                        t = 16 * h + c
                        for col, half in ((F, 0), (F + 1, 1)):
                            last = nc.tensor.matmul(ps[half][:, c // 4, c % 4 * P:(c % 4 + 1) * P],
                                                    HR[:, t, col:col + 1].to_broadcast([P, P]), ident[:, :],
                                                    start=True, stop=True)
                    last.then_inc(sems["bc"], 1)
                pe.wait_ge(sems["att"], n + 1)
                for b in range(9):
                    if b < 8:
                        if b >= 2:
                            pe.wait_ge(sems["copied"], n * 8 + (b - 1))
                        for k in range(4):
                            col = (4 * b + k) * P
                            last = nc.tensor.transpose(ps[0][:, b % 2, k * P:(k + 1) * P], T[:, col:col + P], ident[:, :])
                        last.then_inc(sems["turned"], 1)
                    if b >= 1:
                        c = b - 1
                        pe.wait_ge(sems["copied"], n * 8 + (c + 1))
                        for k in range(4):
                            last = nc.tensor.matmul(ps[1][:, 0, 0:F], attT[:, c % 2, k * P:(k + 1) * P],
                                                    HR[:, 4 * c + k, 0:F], start=(c == 0 and k == 0),
                                                    stop=(c == 7 and k == 3))
                        last.then_inc(sems["summed"], 1)

            pe.wait_ge(hr_ready, 8)
            dense(ds1, 0)
            with pe.If(pe.value_load(flag[0:1, 0:1], min_val=0, max_val=1) > 0):
                pe.wait_ge(ds1["out"], 2)
                pe.sem_inc(gl1["summed"], 1)
                with pe.Fori(0, NT) as t:
                    dense(gl1, t)

        @block.vector
        def _(v):
            own = [0]

            def inc(ins):
                ins.then_inc(dve, 1)
                own[0] += 1
                return own[0]

            def done(ins):
                v.wait_ge(dve, inc(ins))

            v.wait_ge(x_in, 16)
            for t in range(NT):
                inc(v.bn_stats(st6[:, t, :], xs[:, t, :]))
            v.wait_ge(dve, own[0])
            for t in range(NT):
                inc(v.bn_aggr(mv[:, t, :], st6[:, t, :]))
            v.wait_ge(dve, own[0])
            v.sem_inc(stats0, 1)
            v.wait_ge(sd0, 1)
            v.reciprocal(rstd[:, :], sd[:, :]).then_inc(rstd0, 1)
            v.wait_ge(consts, 1)
            for c in range(CPS):
                inc(v.tensor_scalar(diag[:, c, :], ident[:, :], kcol[:, c:c + 1], None, ALU.mult))
            inc(v.tensor_copy(identh[:, :], ident[:, :]))
            done(v.tensor_scalar(rowmask[:, :], rowmask[:, :], float(HUB), None, ALU.is_ge))
            v.sem_inc(consts2, 1)
            v.sem_inc(keys_used, 4)
            v.sem_inc(hub_used, 2)
            v.sem_inc(ds1["out"], 1)

            def spread(g, out_, in_, c1):
                done(v.tensor_tensor(qe[:, 0:c1], in_, nend[g][:, :], ALU.mult))
                done(v.tensor_tensor(qe[:, 0:c1], in_, qe[:, 0:c1], ALU.subtract))
                done(v.tensor_tensor_scan(out_[:, ::-1], nend[g][:, ::-1], qe[:, 0:c1][:, ::-1], 0.0, ALU.mult, ALU.add))

            def accumulate(n):
                l, g, c = CHUNKS[n]
                v.wait_ge(gath[slot(n)], gathered(n))
                if n >= RSLOTS:
                    v.wait_ge(stored[n % RSLOTS], rstored(n - RSLOTS))
                for e in range(CH):
                    at = c * CH + e
                    new = R[:, n % RSLOTS, e, :]
                    old = R[:, (n if e else n - 1) % RSLOTS, (e - 1) % CH, :]
                    row = G[:, slot(n) * CH + e, 0:F]
                    if l:
                        k = K1ST[g] + at
                        v.wait_ge(wg_ready, k + 1)
                        row = WG[:, k % 4, :]
                    if at == 0:
                        ins = v.tensor_copy(new, row)
                    else:
                        ins = v.scalar_tensor_tensor(new, old, cont[g][:, at:at + 1], row, ALU.mult,
                                                     ALU.add if l else ALU.max)
                    if l:
                        ins.then_inc(wg_used, 1)
                        v.wait_ge(wg_used, k + 1)
                    else:
                        done(ins)
                v.sem_inc(chunk_used, 1)

            def lists(t, part):
                g = max(g for g in range(GROUPS) if T0G[g] <= t)
                lk = LIST[g]
                k = K[:, t % 2, :]
                at = LS[g] + (t - max(T0G[g], 1)) * lk
                if part == 0:
                    done(v.tensor_reduce(ovs[:, t:t + 1], k.rearrange("p (s m) -> p s m", m=M8)[:, :, M8 - 1], X, ALU.max))
                elif part == 1:
                    done(v.tensor_tensor(k, k, offs[:, :, :].rearrange("p s m -> p (s m)"), ALU.add))
                elif part < 2 * (lk // M8) + 1:
                    r, what = divmod(part - 2, 2)
                    top = L[:, at + r * M8:at + (r + 1) * M8]
                    if what == 0:
                        done(v.max(top, k))
                    else:
                        done(v.match_replace(k, top, k, 0.0))

            def search(t):
                for bank in range(BANKS):
                    v.wait_ge(keys_ready, t * BANKS + bank + 1)
                    for piece in range(2):
                        s = 2 * bank + piece
                        ins = v.max(K[:, t % 2, s * M8:(s + 1) * M8], ps[0][:, bank, piece * 2 * P:(piece + 1) * 2 * P])
                        if piece:
                            ins.then_inc(keys_used, 1)
                        if t > 1 and t not in T0G:
                            lists(t - 1, s)
                if t > 1 and t not in T0G:
                    lists(t - 1, SEG)
                v.wait_ge(keys_used, (t + 2) * BANKS)

            def finish_list(t):
                for part in range(2 * (max(LIST) // M8) + 1):
                    lists(t, part)

            def search0():
                per = PIECES // SEG
                for bank in range(BANKS):
                    v.wait_ge(keys_ready, bank + 1)
                    for q in range(2 * per):
                        last = v.max(K0[:, (bank * 2 * per + q) * M8:(bank * 2 * per + q + 1) * M8],
                                     ps[0][:, bank, q * (BANK // per // 2):(q + 1) * (BANK // per // 2)])
                    last.then_inc(keys_used, 1)
                v.wait_ge(keys_used, 2 * BANKS)
                done(v.tensor_scalar(K0, K0, rowmask[:, 0:1], None, ALU.mult))
                done(v.tensor_reduce(ovs[:, 0:1], K0.rearrange("p (q m) -> p q m", m=M8)[:, :, M8 - 1], X, ALU.max))
                k0 = K0.rearrange("p (s q m) -> p s q m", s=SEG, m=M8)
                done(v.tensor_tensor(k0, k0, offs[:, :, None, :].to_broadcast([P, SEG, PIECES // SEG, M8]), ALU.add))
                for r in range(LIST0 // M8):
                    done(v.max(L[:, r * M8:(r + 1) * M8], K0))
                    if r + 1 < LIST0 // M8:
                        done(v.match_replace(K0, L[:, r * M8:(r + 1) * M8], K0, 0.0))

            def queue(g):
                T, cap, w = TG[g], CAP[g], LW[g]
                k = L[:, 0:w]
                tiles = L[:, LS[g]:w].rearrange("p (t m) -> p t m", m=LIST[g])
                lf3 = lf[:, LS[g]:w].rearrange("p (t m) -> p t m", m=LIST[g])
                inc(v.tensor_reduce(ovs[:, NT + g:NT + g + 1], tiles[:, :, LIST[g] - 1], X, ALU.max))
                if g == 0:
                    inc(v.tensor_copy(ovs[:, NT + 3 * GROUPS:NT + 3 * GROUPS + 1], L[:, LIST0 - 1:LIST0]))
                inc(v.tensor_copy(li[:, 0:w], k))
                done(v.tensor_scalar(lf[:, 0:w], k, float(M8), None, ALU.is_ge))
                done(v.tensor_scalar(lh[:, 0:w], lf[:, 0:w], float(TILE), None, ALU.mult))
                lh3 = lh[:, LS[g]:w].rearrange("p (t m) -> p t m", m=LIST[g])
                inc(v.tensor_scalar(lw[:, 0:w], li[:, 0:w], 24, None, ALU.bitwise_and))
                done(v.tensor_tensor(lh3, lh3, tnum[:, T - TL[g]:T, None].to_broadcast([P, TL[g], LIST[g]]), ALU.mult))
                done(v.tensor_tensor(tiles, tiles, lh3, ALU.add))
                inc(v.tensor_scalar(lsec[:, 0:w], lw[:, 0:w], 24.0, None, ALU.is_equal))
                done(v.tensor_scalar(li[:, 0:w], li[:, 0:w], TILE - M8, None, ALU.bitwise_and))
                inc(v.tensor_tensor(lf[:, 0:w], lf[:, 0:w], lsec[:, 0:w], ALU.add))
                done(v.tensor_scalar(lh[:, 0:w], li[:, 0:w], 8.0, 0.5, ALU.add, ALU.mult))
                inc(v.tensor_reduce(cnt[g][:, T - TL[g]:T], lf3, X, ALU.add))
                if g == 0:
                    inc(v.tensor_reduce(cnt[0][:, 0:1], lf[:, 0:LIST0], X, ALU.add))
                v.wait_ge(dve, own[0])
                inc(v.tensor_tensor(lf[:, 0:w], k, lh[:, 0:w], ALU.subtract))
                done(v.tensor_tensor(lh[:, 0:w], lh[:, 0:w], lsec[:, 0:w], ALU.mult))
                inc(v.tensor_tensor(k, k, lh[:, 0:w], ALU.subtract))
                done(v.scalar_tensor_tensor(lsec[:, 0:w], lf[:, 0:w], 8.0, lsec[:, 0:w], ALU.add, ALU.mult))
                for r in range(BOTH // M8):
                    two = L[:, w + r * M8:w + (r + 1) * M8]
                    done(v.max(two, lsec[:, 0:w]))
                    if r + 1 < BOTH // M8:
                        done(v.match_replace(lsec[:, 0:w], two, lsec[:, 0:w], 0.0))
                inc(v.tensor_copy(ovs[:, NT + GROUPS + g:NT + GROUPS + g + 1], L[:, w + BOTH - 1:w + BOTH]))
                k = L[:, 0:w + BOTH]
                for r in range(cap // M8):
                    done(v.max(Q[:, r * M8:(r + 1) * M8], k))
                    if r + 1 < cap // M8:
                        done(v.match_replace(k, Q[:, r * M8:(r + 1) * M8], k, 0.0))
                q_ = Q[:, 0:cap]
                inc(v.tensor_copy(ovs[:, NT + 2 * GROUPS + g:NT + 2 * GROUPS + g + 1], Q[:, cap - 1:cap]))
                inc(v.tensor_scalar(pad[:, 0:cap], q_, float(M8), float(2 * N), ALU.is_lt, ALU.mult))
                done(v.tensor_copy(qi[:, 0:cap], q_))
                inc(v.tensor_scalar(qn[:, 0:cap], qi[:, 0:cap], 2, N // 2 - 8, ALU.logical_shift_right, ALU.bitwise_and))
                inc(v.tensor_scalar(qb[:, 0:cap], qi[:, 0:cap], 16, 7, ALU.bitwise_and, ALU.logical_shift_left))
                done(v.tensor_scalar(idx[g][:, :], qi[:, 0:cap], 7, None, ALU.bitwise_and))
                done(v.tensor_tensor(qn[:, 0:cap], qn[:, 0:cap], qb[:, 0:cap], ALU.bitwise_or))
                done(v.tensor_tensor(idx[g][:, :], idx[g][:, :], qn[:, 0:cap], ALU.bitwise_or))
                done(v.tensor_tensor(idx[g][:, :], idx[g][:, :], pad[:, 0:cap], ALU.add))
                v.sem_inc(queue_ready, 1)
                inc(v.tensor_scalar(qe[:, 0:cap], q_, float(M8), None, ALU.is_lt))
                done(v.tensor_scalar(qn[:, 0:cap], qi[:, 0:cap], TILE.bit_length() - 1, None, ALU.logical_shift_right))
                done(v.tensor_tensor(tf[g][:, :], qn[:, 0:cap], qe[:, 0:cap], ALU.subtract))
                inc(v.memset(cont[g][:, 0:1], 0.0))
                inc(v.tensor_tensor(cont[g][:, 1:], tf[g][:, 1:], tf[g][:, 0:cap - 1], ALU.is_equal))
                done(v.tensor_tensor_scan(pre[:, 0:T], onesr[:, 0:T], cnt[g][:, :], 0.0, ALU.mult, ALU.add))
                done(v.tensor_tensor(ef[:, 0:T], cnt[g][:, :], pre[:, 0:T], ALU.subtract))
                done(v.tensor_scalar(ef[:, 0:T], ef[:, 0:T], pre[:, T - 1:T], None, ALU.add))
                if g == 0:
                    done(v.tensor_scalar(ovt[:, 0:1], ef[:, 1:2], float(CAP1[0]), None, ALU.is_gt))
                done(v.tensor_scalar(ef[:, 0:T], ef[:, 0:T], pcol[:, g:g + 1], None, ALU.add))
                done(v.tensor_scalar(pre[:, 0:T], cnt[g][:, :], 0.5, float(P * N), ALU.is_lt, ALU.mult))
                done(v.tensor_tensor(ef[:, 0:T], ef[:, 0:T], pre[:, 0:T], ALU.add))
                done(v.tensor_scalar(eidx[g][:, :], ef[:, 0:T], float(P * CAP[g]), None, ALU.min))

            def queue1(g):
                c1 = CAP1[g]
                inc(v.memset(nend[g][:, c1 - 1:c1], 0.0))
                inc(v.tensor_copy(nend[g][:, 0:c1 - 1], cont[g][:, 1:c1]))
                inc(v.tensor_scalar(reset[g][:, :], cont[g][:, 0:c1], BIG, -BIG, ALU.mult, ALU.add))
                done(v.tensor_tensor_scan(nq[g][:, :], cont[g][:, 0:c1], onesr[:, 0:c1], 0.0, ALU.mult, ALU.add))
                spread(g, nq[g][:, :], nq[g][:, :], c1)

            search0()
            behind = 0
            for t in range(1, NT):
                if t in T0G:
                    g = T0G.index(t)
                    finish_list(t - 1)
                    queue(g - 1)
                search(t)
                if t >= NT - BEHIND:
                    accumulate(behind)
                    behind += 1
            finish_list(NT - 1)
            queue(GROUPS - 1)

            v.wait_ge(stage_used, NT + 1)
            inc(v.tensor_reduce(ovt[:, 1:2], ovs[:, :], X, ALU.max))
            inc(v.tensor_reduce(ovt[:, 2:3], sgn[:, :], X, ALU.add))
            for g in range(GROUPS):
                inc(v.tensor_reduce(ovt[:, 3 + g:4 + g], cnt[g][:, :], X, ALU.add))
            v.wait_ge(dve, own[0])
            done(v.tensor_scalar(ovt[:, 1:2], ovt[:, 1:2], float(M8), None, ALU.is_ge))
            inc(v.tensor_tensor(ovd[:, 0:1], ovt[:, 0:1], ovt[:, 1:2], ALU.add))
            done(v.tensor_reduce(ovt[:, 3:4], ovt[:, 3:3 + GROUPS], X, ALU.add))
            done(v.tensor_tensor(ovd[:, 1:2], ovt[:, 3:4], ovt[:, 2:3], ALU.subtract))
            v.sem_inc(diffs, 1)

            v.wait_ge(adjn_in, 16)
            v.tensor_scalar(maskn, adjn, 0.0, None, ALU.not_equal).then_inc(maskn_ready, 1)

            def hub_half(n, h, ready, used, to):
                v.wait_ge(ready, n + 1)
                v.wait_ge(used, n + 2)
                if not isinstance(n, int):
                    v.sem_inc(passed_v, 1)
                v.tensor_tensor_reduce(out=junk[:, 0:2048], in0=ps[h][:, :, :].rearrange("p b n -> p (b n)"),
                                       in1=HT[:, h * 2048:(h + 1) * 2048], scale=1.0,
                                       scalar=hm[:, 0:1] if h else 0.0, op0=ALU.mult, op1=ALU.max,
                                       accum_out=to if h else hm[:, 0:1]).then_inc(used, 1)

            v.wait_ge(h0t_used, 8)
            done(v.memset(aggT, 0.0))
            hubs = 0

            left = L0CH - BEHIND
            for m, n in enumerate(range(BEHIND, L0CH)):
                accumulate(n)
                while hubs < 2 * HUB and hubs * left < (m + 1) * 2 * HUB:
                    hub_half(hubs, hubs % 2, hubp, hub_used, aggT[:, hubs // 2:hubs // 2 + 1])
                    hubs += 1
            v.wait_ge(hub_used, 2 * HUB + 2)
            v.sem_inc(hub_done, 1)
            v.wait_ge(flag_sum, 1)
            done(v.tensor_scalar(flagf[:, :], ps[1][0:1, 1, 0:2], 0.0, None, ALU.not_equal))
            v.tensor_tensor(flag[:, :], flagf[:, 0:1], flagf[:, 1:2], ALU.max).then_inc(flag_ready, 1)
            v.wait_ge(hub_t, 1)
            v.wait_ge(ends[0][0], 16 * 4)
            done(v.tensor_copy(A[0:HUB, 0, :], ps[1][0:HUB, 0, 0:P]))

            v.wait_ge(flag_ready, 1)
            with v.If(v.value_load(flag[0:1, 0:1], min_val=0, max_val=1) > 0):
                for b in range(8):
                    v.wait_ge(ends[0][b], 16 * 4)
                v.sem_inc(gl0["used"], 2)
                v.sem_inc(gl0["done"], 1)
                with v.Fori(0, NT) as t:
                    v.wait_ge(gl0["in"], (t + 1) * 16)
                    v.tensor_scalar(maskn, adjn, 0.0, None, ALU.not_equal).then_inc(gl0["mask"], 1)
                    with v.Fori(0, P) as i:
                        r = v.snap(t * P + i)
                        for h in range(2):
                            hub_half(r * 2 + h, h, gl0["p"], gl0["used"], hm[:, 1:2])
                        v.wait_ge(gl0["used"], r * 2 + 4)
                        v.tensor_copy(aggT[:, bass.ds(i, 1)], hm[:, 1:2]).then_inc(gl0["own"], 1)
                        v.wait_ge(gl0["own"], r + 1)
                    v.wait_ge(gl0["t"], t + 1)
                    v.tensor_copy(A[:, bass.ds(t, 1), :].rearrange("p a f -> p (a f)"),
                                  ps[0][:, 0, 0:P]).then_inc(gl0["done"], 1)
                v.wait_ge(gl0["done"], NT + 1)

            def head(b):
                ts = slice(4 * b, 4 * b + 4)
                v.wait_ge(ends[0][b], 16 * 4)
                done(v.tensor_tensor(xs[:, ts, :], xs[:, ts, :], A[:, ts, :], ALU.add))
                for t in range(4 * b, 4 * b + 4):
                    inc(v.bn_stats(st6[:, t, :], xs[:, t, :]))
                v.wait_ge(dve, own[0])
                for t in range(4 * b, 4 * b + 4):
                    inc(v.bn_aggr(mv[:, t, :], st6[:, t, :]))
                v.wait_ge(dve, own[0])
                v.sem_inc(var1, 1)
                v.wait_ge(sd1, b + 1)
                done(v.reciprocal(rstd[:, ts], sd[:, ts]))
                if b:
                    v.wait_ge(xnt, b)
                for k in range(4):
                    t = 4 * b + k
                    inc(v.tensor_scalar(xn[:, k, :], xs[:, t, :], mv[:, t, 0:1], rstd[:, t:t + 1], ALU.subtract, ALU.mult))
                v.wait_ge(dve, own[0])
                v.sem_inc(xn_ready, 1)

            def tail(b):
                ts = slice(4 * b, 4 * b + 4)
                v.wait_ge(hr_copied, 4 * b + 4)
                sd_ = ps[0][:, 2, 0:8].rearrange("p (k c) -> p k c", c=2)
                inc(v.tensor_copy(S[:, ts], sd_[:, :, 0]))
                inc(v.tensor_copy(HR[:, ts, F], sd_[:, :, 1]))
                inc(v.tensor_scalar(HR[:, ts, F + 1], hsum[:, ts], 0.0, None, ALU.not_equal))
                done(v.memset(HR[:, ts, F + 2:ROW], 0.0))
                v.sem_inc(hr_ready, 1)

            for b in range(8):
                head(b)
                if b:
                    tail(b - 1)
            tail(7)

            def dense(sems, n, tile):
                steps = 14

                def mine(k, ins):
                    ins.then_inc(sems["own"], 1)
                    v.wait_ge(sems["own"], n * steps + k)

                v.tensor_copy(dn[:, 0:1], S[:, tile]).then_inc(sems["score"], 1)
                v.wait_ge(sems["in"], (n + 1) * 16)
                for h in range(2):
                    cols = slice(h * 2048, (h + 1) * 2048)
                    v.wait_ge(sems["bc"], n * 2 + (h + 1))
                    v.scalar_tensor_tensor(V[:, cols], adjn[:, cols], 0.0, ps[1][:, :, :].rearrange("p b n -> p (b n)"),
                                           ALU.is_gt, ALU.mult, accum_out=dn[:, 1 + h:2 + h]).then_inc(sems["bc_dve"], 1)
                v.wait_ge(sems["bc_dve"], n * 2 + 2)
                v.wait_ge(sems["bc_act"], n * 2 + 2)
                mine(1, v.tensor_tensor(dn[:, 5:6], dn[:, 1:2], dn[:, 2:3], ALU.add))
                mine(2, v.scalar_tensor_tensor(U, U, ALPHA, U, ALU.mult, ALU.max))
                mine(3, v.tensor_tensor(U, U, V, ALU.mult))
                mine(4, v.tensor_scalar(T, V, -NEG, NEG, ALU.mult, ALU.add))
                mine(5, v.tensor_tensor(U, U, T, ALU.add))
                mine(6, v.tensor_reduce(dn[:, 6:7], U, X, ALU.max))
                mine(7, v.tensor_scalar(dn[:, 3:4], dn[:, 6:7], -1.0, None, ALU.mult))
                v.sem_inc(sems["masked"], 1)
                v.wait_ge(sems["exp"], n + 1)
                mine(8, v.reciprocal(dn[:, 8:9], dn[:, 4:5]))
                mine(9, v.scalar_tensor_tensor(U, U, dn[:, 8:9], V, ALU.mult, ALU.mult))
                mine(10, v.tensor_reduce(dn[:, 6:7], U, X, ALU.max))
                mine(11, v.tensor_scalar(dn[:, 7:8], dn[:, 6:7], THR, None, ALU.is_gt))
                mine(12, v.tensor_tensor(dn[:, 7:8], dn[:, 7:8], dn[:, 5:6], ALU.mult))
                mine(13, v.scalar_tensor_tensor(T, U, THR, U, ALU.is_ge, ALU.mult))
                v.sem_inc(sems["att"], 1)
                v.wait_ge(sems["summed"], n * 8 + 9)
                mine(14, v.tensor_scalar(A[:, tile, :].rearrange("p a f -> p (a f)"), ps[1][:, 0, 0:F],
                                         dn[:, 7:8], None, ALU.mult))
                v.sem_inc(sems["out"], 1)

            dense(ds1, 0, slice(0, 1))

            for g in ORDER[1]:
                queue1(g)
                c1 = CAP1[g]
                done(v.memset(sq[g], 0.0))
                for t in range(T0G[g] == 0, TG[g]):
                    tile = T0G[g] + t
                    done(v.tensor_scalar(qe[:, 0:c1], tf[g][:, 0:c1], float(t), S[:, tile:tile + 1], ALU.is_equal, ALU.mult))
                    done(v.tensor_tensor(sq[g], sq[g], qe[:, 0:c1], ALU.add))

            def weights(g):
                nth, c1 = ORDER[1].index(g), CAP1[g]
                D, VV, u, m, ex, exn, z, top = (qv[:, k, 0:c1] for k in range(8))
                for c in range(NCH[1][g]):
                    n = FIRST[1, g] + c
                    v.wait_ge(gath[slot(n)], gathered(n))
                    inc(v.tensor_copy(qv[:, 0, c * CH:(c + 1) * CH], G[:, slot(n) * CH:(slot(n) + 1) * CH, F]))
                    inc(v.tensor_copy(qv[:, 1, c * CH:(c + 1) * CH], G[:, slot(n) * CH:(slot(n) + 1) * CH, F + 1]))
                v.wait_ge(dve, own[0])
                inc(v.scalar_tensor_tensor(VV, tf[g][:, 0:c1], float(T0G[g] == 0), VV, ALU.is_ge, ALU.mult))
                done(v.tensor_tensor(u, D, sq[g], ALU.add))
                inc(v.tensor_scalar(D, nq[g][:, :], -1.0, float(N), ALU.mult, ALU.add))
                done(v.scalar_tensor_tensor(u, u, ALPHA, u, ALU.mult, ALU.max))
                inc(v.tensor_scalar(z, VV, -NEG, NEG, ALU.mult, ALU.add))
                done(v.tensor_tensor(u, u, VV, ALU.mult))
                done(v.tensor_tensor(u, u, z, ALU.add))
                done(v.tensor_tensor_scan(m, reset[g][:, :], u, -BIG, ALU.add, ALU.max))
                spread(g, m, m, c1)
                done(v.tensor_scalar(m, m, NEG, None, ALU.max))
                inc(v.tensor_tensor(ex, u, m, ALU.subtract))
                done(v.tensor_scalar(exn, m, -1.0, NEG, ALU.mult, ALU.add))
                v.sem_inc(exq, 1)
                done(v.tensor_tensor_scan(top, cont[g][:, 0:c1], VV, 0.0, ALU.mult, ALU.add))
                spread(g, wq[g], top, c1)
                v.wait_ge(exq_done, nth + 1)
                inc(v.tensor_tensor(D, D, exn, ALU.mult))
                done(v.tensor_tensor_scan(z, cont[g][:, 0:c1], ex, 0.0, ALU.mult, ALU.add))
                spread(g, z, z, c1)
                done(v.tensor_tensor(z, z, D, ALU.add))
                inc(v.tensor_tensor(ex, ex, VV, ALU.mult))
                done(v.reciprocal(z, z))
                done(v.tensor_tensor(ex, ex, z, ALU.mult))
                done(v.tensor_tensor_scan(top, cont[g][:, 0:c1], ex, 0.0, ALU.mult, ALU.max))
                spread(g, top, top, c1)
                done(v.scalar_tensor_tensor(ex, ex, THR, ex, ALU.is_ge, ALU.mult))
                done(v.scalar_tensor_tensor(ex, top, THR, ex, ALU.is_gt, ALU.mult))
                done(v.tensor_tensor(wq[g], wq[g], ex, ALU.mult))
                v.sem_inc(w_ready, 1)

            def elu_head(sems, b):
                ts = slice(4 * b, 4 * b + 4)
                done(v.tensor_tensor(Z[:, ts, :], HR[:, ts, 0:F], A[:, ts, :], ALU.add))
                done(v.tensor_scalar(EZ[:, ts, :], Z[:, ts, :], 0.0, None, ALU.min))
                v.sem_inc(sems["z"], 1)

            def elu_tail(sems, n, b):
                ts = slice(4 * b, 4 * b + 4)
                v.wait_ge(sems["ez"], n + 1)
                done(v.scalar_tensor_tensor(Z[:, ts, :], Z[:, ts, :], 0.0, EZ[:, ts, :], ALU.max, ALU.add))
                done(v.scalar_tensor_tensor(O[:, ts, :], Z[:, ts, :], -1.0, xs[:, ts, :], ALU.add, ALU.add))
                v.sem_inc(sems["o"], 1)

            def elus(sems, order, first, count):
                for n in range(first, first + count + 1):
                    if n < first + count:
                        if sems is elu:
                            b = order[n]
                            v.wait_ge(ends[1][b], 16 * (3 if b == 0 else 4))
                        elu_head(sems, order[n])
                    if n > first:
                        elu_tail(sems, n - 1, order[n - 1])

            n_first = len(BATCHES[ORDER[1][0]])
            for nth, g in enumerate(ORDER[1]):
                if nth == 2:
                    elus(elu, ELU, 0, n_first)
                weights(g)
                for n in range(FIRST[1, g], FIRST[1, g] + NCH[1][g]):
                    accumulate(n)
            elus(elu, ELU, n_first, 8 - n_first)

            with v.If(v.value_load(flag[0:1, 0:1], min_val=0, max_val=1) > 0):
                v.wait_ge(elu["in"], 16 * 8)
                v.sem_inc(gl1["out"], 1)
                with v.Fori(0, NT) as t:
                    dense(gl1, t, bass.ds(t, 1))
                v.wait_ge(gl1["out"], NT + 1)
                elus(gelu, range(8), 0, 8)


def kernel(x, adj, L1_gnn_W, L1_gnn_a):
    import numpy as np
    from concourse import bacc
    from concourse.bass_utils import run_bass_kernel_spmd

    x, adj, w, a = (np.ascontiguousarray(v) for v in (x, adj, L1_gnn_W, L1_gnn_a))
    adj_t = np.ascontiguousarray(adj.reshape(NT, P, CPS, P, SEG).transpose(0, 3, 4, 2, 1)).reshape(NT * P, N)
    a = np.ascontiguousarray(a.reshape(2, F).T)
    nc = bacc.Bacc("TRN2", target_bir_lowering=False, num_devices=1)
    arrays, args = {}, []
    for name, v in (("x", x), ("adj", adj), ("adj_t", adj_t), ("w", w), ("a", a)):
        arrays[f"in_{name}"] = v
        args.append(nc.dram_tensor(f"in_{name}", v.shape, mybir.dt.from_np(v.dtype), kind="ExternalInput").ap())
    args.append(nc.dram_tensor("out", (N, F), f32, kind="ExternalOutput").ap())
    build(nc, *args)
    return run_bass_kernel_spmd(nc, [arrays], core_ids=[0]).results[0]["out"]
```

```python
from contextlib import ExitStack

import concourse.bass as bass
from concourse import mybir

N, F, P = 4096, 128, 128
NT = N // P
SEG = 8
CPS = N // SEG // P
M8 = 8
HUB = 6
PIECES = 64
GROUPS = 3
T0G = (0, 4, 20)
TG = (4, 16, 12)
CAP = (88, 84, 48)
CAP1 = (44, 84, 48)
ORDER = ((0, 1, 2), (1, 2, 0))
LISTS = ((0, 32), (4, 24), (6, 16))
LIST0 = 64
PARTS = ((0,), (4, 10), (20, 30))
BOTH = 8
TILE = 1 << 14
CH = 8
CHUNK_TILE = tuple(range(21, 32))
BEHIND = len(CHUNK_TILE)
TURNS = 15
SLOTS = 14
RSLOTS = 4
ROW = 130
STAGES = 3
BANK = 512
EARLY = 11
HUB_TILES = range(EARLY, EARLY + 2 * HUB)
HUB_SLOT = 9
BANKS = 4
EPS, ALPHA, THR, NEG, BIG = 1e-5, 0.2, 1e-4, -1e9, 3e38

DENSE = ("in", "score", "bc", "bc_act", "bc_dve", "masked", "exp", "att", "turned", "copied", "summed", "own", "out")

f32, f16, i32 = mybir.dt.float32, mybir.dt.float16, mybir.dt.int32
ALU = mybir.AluOpType
ACT = mybir.ActivationFunctionType
X = mybir.AxisListType.X


def build(nc, x, adj, adj_t, w, a, out):
    t0 = nc.dram_tensor("h0_rows", [N, F], f32, kind="Internal").ap()
    t1 = nc.dram_tensor("h_rows", [N, ROW], f32, kind="Internal").ap()
    run = [nc.dram_tensor(f"running{g}", [P * CAP[g] + 1, F], f32, kind="Internal").ap() for g in range(GROUPS)]

    ctx = ExitStack()
    with ctx:
        def sb(name, shape, dt=f32):
            return ctx.enter_context(nc.sbuf_tensor(name, shape, dt))

        def sem(name):
            return ctx.enter_context(nc.semaphore(name))

        xs = sb("xs", [P, NT, F])
        G = sb("gathered", [P, SLOTS * CH, ROW])
        R = sb("running", [P, RSLOTS, CH, F])
        h0 = R[:, :, :, :].rearrange("p s e f -> p (s e) f")
        HT = sb("h0_transposed", [P, N])[:, :]
        arena = sb("arena", [P, 18432])
        AT = 2 * N + NT * ROW
        stage = [arena[:, s * N:(s + 1) * N].bitcast(i32) for s in range(STAGES)]
        mask = [arena[:, 3 * N + s * N // 2:3 * N + (s + 1) * N // 2].bitcast(f16) for s in range(STAGES)]
        adjn = arena[:, 0:N].bitcast(i32)
        maskn = arena[:, N:N + N // 2].bitcast(f16)
        junk = arena[:, N + N // 2:2 * N]
        V = arena[:, 0:N]
        U = arena[:, N:2 * N]
        T = HT
        HR = arena[:, 2 * N:2 * N + NT * ROW].rearrange("p (t c) -> p t c", c=ROW)
        A = arena[:, AT:AT + N].rearrange("p (t f) -> p t f", f=F)
        work = sb("work", [P, 2 * BANK + 8 * F])
        attT = work[:, 0:2 * BANK].rearrange("p (b n) -> p b n", b=2)
        hTs = attT
        xn = work[:, 2 * BANK:].rearrange("p (b k f) -> p b k f", b=2, f=F)
        hubmask = work[0:HUB, 0:N // 2].bitcast(f16)
        hub_stage = G[0:HUB, HUB_SLOT * CH:(HUB_SLOT + 4) * CH, :].rearrange("p r c -> p (r c)")[:, 0:N].bitcast(i32)
        ident = sb("ident", [P, P])
        identh = sb("identh", [P, P], f16)
        diag = sb("diag", [P, CPS, P], f16)
        kcol = sb("kcol", [P, CPS])
        ones = sb("ones", [P, 1])
        rowmask = sb("rowmask", [P, 1])
        pcol = sb("pcol", [P, GROUPS])
        offs = sb("offs", [P, SEG, M8])
        tnum = sb("tnum", [P, max(TG)])
        qv = sb("qv", [P, 8, max(CAP1)])
        K0 = qv[:, :, :].rearrange("p a b -> p (a b)")[:, 0:PIECES * M8]
        K = sb("K", [P, 2, SEG * M8])
        LS = [LIST0 if g == 0 else 0 for g in range(GROUPS)]
        LIST = [max(k for first, k in LISTS if first <= t and all(f <= first or f > t for f, _ in LISTS))
                for t in range(NT)]
        AT_LIST = [LS[g] + sum(LIST[max(T0G[g], 1):t]) for g in range(GROUPS) for t in range(T0G[g], T0G[g] + TG[g])]
        LW = [AT_LIST[T0G[g] + TG[g] - 1] + LIST[T0G[g] + TG[g] - 1] for g in range(GROUPS)]
        LQ = [LW[g] + BOTH * len(PARTS[g]) for g in range(GROUPS)]
        L_first = sb("L_first", [P, LQ[0]])
        L_rest = sb("L_rest", [P, max(LQ[1:])])
        L = [L_rest if g else L_first for g in range(GROUPS)]
        LB = max(LW)
        li = sb("li", [P, LB], i32)
        lw = sb("lw", [P, LB], i32)
        lf = sb("lf", [P, LB])
        lh = sb("lh", [P, LB])
        lsec = lw[:, :].bitcast(f32)
        cnt = [sb(f"cnt{g}", [P, TG[g]]) for g in range(GROUPS)]
        pre = sb("pre", [P, max(TG)])
        Q = sb("Q", [P, max(CAP)])
        qi = sb("qi", [P, max(CAP)], i32)
        qn = sb("qn", [P, max(CAP)], i32)
        qb = sb("qb", [P, max(CAP)], i32)
        pad = sb("pad", [P, max(CAP)], i32)
        idx = [sb(f"idx{g}", [P, CAP[g]], i32) for g in range(GROUPS)]
        tf = [sb(f"tf{g}", [P, CAP[g]]) for g in range(GROUPS)]
        cont = [sb(f"cont{g}", [P, CAP[g]]) for g in range(GROUPS)]
        ef = sb("ef", [P, max(TG)])
        eidx = [sb(f"eidx{g}", [P, TG[g]], i32) for g in range(GROUPS)]
        nend = [sb(f"nend{g}", [P, CAP1[g]]) for g in range(GROUPS)]
        reset = [sb(f"reset{g}", [P, CAP1[g]]) for g in range(GROUPS)]
        nq = [sb(f"nq{g}", [P, CAP1[g]]) for g in range(GROUPS)]
        sgn = sb("sgn", [P, NT])
        ovs = sb("ovs", [P, 64])
        ovd = sb("ovd", [P, 2])
        flagf = sb("flagf", [1, 2])
        flag = sb("flag", [1, 1], i32)
        st6 = sb("st6", [P, NT, 6])
        mv = sb("mv", [P, NT, 2])
        sd = sb("sd", [P, NT])
        rstd = sb("rstd", [P, NT])
        epsb = sb("epsb", [P, 1])
        hm = sb("hm", [P, 4])
        Ws = sb("Ws", [P, F + 2])
        WT = work[:, 0:F]
        a2 = sb("a2", [P, 2])
        S = sb("S", [P, NT])
        hsum = sb("hsum", [P, NT])
        tail_ = arena[:, AT + N:]
        WG = tail_[:, 0:4 * F].rearrange("p (k f) -> p k f", f=F)
        aggT = sb("aggregates_transposed", [P, P])[:, :]
        sq = [tail_[:, 5 * F + g * P:5 * F + g * P + CAP1[g]] for g in range(GROUPS)]
        wq = [tail_[:, 8 * F + g * P:8 * F + g * P + CAP1[g]] for g in range(GROUPS)]
        dn = sb("dn", [P, 12])
        zrow = sb("zrow", [1, F])
        onesr = sb("onesr", [P, max(CAP1)])
        qe = sb("qe", [P, max(CAP)])
        ovt = sb("ovt", [P, 4 + GROUPS])
        Z, EZ, O = (v_.rearrange("p (t f) -> p t f", f=F) for v_ in (U, T, V))

        def turned_rows(b):
            return ps[0][:, b % 2, :]

        def product(b, k):
            return ps[1][:, 2 * (b % 2) + k // 2, k % 2 * (F + 2):(k % 2 + 1) * (F + 2)]

        ps = [ctx.enter_context(nc.psum_tensor(f"ps{b}", [P, 4, BANK], f32)) for b in range(2)]

        x_in = sem("x_in"); w_in = sem("w_in")
        adj_in = [sem(f"adj_in{s}") for s in range(STAGES)]
        stage_used = sem("stage_used")
        mask_used = sem("mask_used")
        keys_ready = sem("keys_ready")
        keys_used = sem("keys_used")
        last_mask = sem("last_mask")
        consts = sem("consts"); consts2 = sem("consts2")
        dve = sem("dve")
        pool = sem("pool")
        stats0 = sem("stats0"); centred = sem("centred"); sd0 = sem("sd0"); rstd0 = sem("rstd0"); h0_ready = sem("h0_ready")
        t0_in = sem("t0_in")
        h0t_ready = sem("h0t_ready"); h0t_used = sem("h0t_used")
        queue_ready = sem("queue_ready")
        gath = [sem(f"gath{s}") for s in range(SLOTS)]
        chunk_used = sem("chunk_used")
        stored = [sem(f"stored{s}") for s in range(RSLOTS)]
        zrow_in = sem("zrow_in")
        ends = [[sem(f"ends{l}_{b}") for b in range(8)] for l in range(2)]
        rows = {n: sem(f"rows_{n}") for n in ("var", "sd", "scale", "centred", "turned", "relu", "h", "copied", "ready")}
        hub_in = sem("hub_in"); hub_sign = sem("hub_sign"); hubmask_ready = sem("hubmask_ready")
        hubp = sem("hubp"); hub_used = sem("hub_used"); hub_t = sem("hub_t")
        flag_sum = sem("flag_sum"); flag_ready = sem("flag_ready"); diffs = sem("diffs")
        wprep = sem("wprep"); wprep_c = sem("wprep_c")
        t1_in = sem("t1_in")
        exq = sem("exq"); exq_done = sem("exq_done"); w_ready = sem("w_ready")
        wg_ready = sem("wg_ready"); wg_used = sem("wg_used")
        ds1 = {n: sem(f"d_{n}") for n in DENSE}
        gl0 = {n: sem(f"g0_{n}") for n in ("in", "mask", "p", "used", "own", "t", "done")}
        gl1 = {n: sem(f"g1_{n}") for n in DENSE}
        ELUS = ("z", "neg", "ez", "y", "o", "in")
        elu = {n: sem(f"elu_{n}") for n in ELUS}
        gelu = {n: sem(f"gelu_{n}") for n in ELUS}

        passed_v = sem("passed_v"); passed_pe = sem("passed_pe")

        block = ctx.enter_context(nc.Block())

        adjt_v = adj_t.rearrange("(t p) n -> t p n", p=P)
        adj_v = adj.rearrange("(t p) n -> t p n", p=P)
        x_v = x.rearrange("(t p) f -> p t f", p=P)
        out_v = out.rearrange("(t p) f -> p t f", p=P)
        t0_v = t0.rearrange("(t p) f -> p t f", p=P)
        t1_v = t1.rearrange("(t p) c -> p t c", p=P)

        NCH = [[-(-cap[g] // CH) for g in range(GROUPS)] for cap in (CAP, CAP1)]
        CHUNKS = [(l, g, c) for l in range(2) for g in ORDER[l] for c in range(NCH[l][g])]
        FIRST = {(l, g): CHUNKS.index((l, g, 0)) for l in range(2) for g in range(GROUPS)}
        L0CH = sum(NCH[0])
        ELU = [b for g in ORDER[1] for b in range(T0G[g] // 4, (T0G[g] + TG[g]) // 4)]
        K1ST = {g: sum(CAP1[m] for m in ORDER[1][:ORDER[1].index(g)]) for g in range(GROUPS)}

        def rounds(n):
            l, g, c = CHUNKS[n]
            return min(CH, (CAP, CAP1)[l][g] - c * CH)

        def slot(n):
            return n % SLOTS

        def gathered(n):
            return 16 * sum(rounds(m) for m in range(n % SLOTS, n + 1, SLOTS))

        def rstored(n):
            return 16 * (n // RSLOTS + 1)

        def store_chunk(queue, n):
            l, g, c = CHUNKS[n]
            queue.wait_ge(chunk_used, n + 1)
            dst = run[g][0:P * CAP[g], :].rearrange("(p q) f -> p q f", p=P)
            queue.dma_start(dst[:, c * CH:c * CH + rounds(n), :], R[:, n % RSLOTS, 0:rounds(n), :]).then_inc(stored[n % RSLOTS], 16)

        @block.sync
        def _(sp):
            sp.dma_start(xs[:, :, :], x_v).then_inc(x_in, 16)
            for t in range(2):
                sp.dma_start(stage[t], adjt_v[t]).then_inc(adj_in[t], 16)
            sp.dma_start(Ws[:, 0:F], w).then_inc(w_in, 16)
            sp.dma_start(a2[:, :], a).then_inc(w_in, 16)
            with sp.Fori(0, (NT - 2) // STAGES) as i:
                for k in range(STAGES):
                    s = (2 + k) % STAGES
                    sp.wait_ge(stage_used, i * STAGES + (k + 1))
                    sp.dma_start(stage[s], adjt_v[i * STAGES + (2 + k)]).then_inc(adj_in[s], 16)

            store_chunk(sp, BEHIND - 1)
            sp.wait_ge(consts2, 1)
            for g in range(GROUPS):
                sp.dma_start(run[g][P * CAP[g]:P * CAP[g] + 1, :], zrow[:, :]).then_inc(zrow_in, 16)

            for n in range(BEHIND, L0CH):
                store_chunk(sp, n)
            sp.wait_ge(flag_ready, 1)
            with sp.If(sp.value_load(flag[0:1, 0:1], min_val=0, max_val=1) > 0):
                with sp.Fori(0, NT) as t:
                    sp.wait_ge(gl0["done"], t + 1)
                    sp.dma_start(adjn, adj_v[t]).then_inc(gl0["in"], 16)
                sp.wait_ge(gl0["done"], NT + 1)
            for b in range(8):
                sp.wait_ge(rows["ready"], b + 1)
                sp.dma_start(t1_v[:, 4 * b:4 * b + 4, :], HR[:, 4 * b:4 * b + 4, :]).then_inc(t1_in, 16)
            sp.dma_start(adjn, adj_v[0]).then_inc(ds1["in"], 16)
            for n in range(L0CH, len(CHUNKS)):
                store_chunk(sp, n)

            def store_out(sems, order):
                for n, b in enumerate(order):
                    sp.wait_ge(sems["o"], n + 1)
                    sp.dma_start(out_v[:, 4 * b:4 * b + 4, :], O[:, 4 * b:4 * b + 4, :]).then_inc(sems["in"], 16)
                sp.wait_ge(sems["in"], 16 * 8)

            store_out(elu, ELU)
            with sp.If(sp.value_load(flag[0:1, 0:1], min_val=0, max_val=1) > 0):
                with sp.Fori(0, NT) as t:
                    sp.wait_ge(gl1["out"], t + 1)
                    sp.dma_start(adjn, adj_v[t]).then_inc(gl1["in"], 16)
                store_out(gelu, range(8))

        @block.gpsimd
        def _(gp):
            own = [0]

            def step(ins):
                ins.then_inc(pool, 1)
                own[0] += 1
                return own[0]

            step(gp.memset(ident[:, :], 0.0))
            step(gp.iota(kcol[:, :], [[8, 2], [32 * P, 2]], base=8, channel_multiplier=32, allow_small_or_imprecise_dtypes=True))
            step(gp.iota(rowmask[:, :], [[0, 1]], base=0, channel_multiplier=1, allow_small_or_imprecise_dtypes=True))
            for g in range(GROUPS):
                step(gp.iota(pcol[:, g:g + 1], [[0, 1]], base=-1, channel_multiplier=CAP[g],
                             allow_small_or_imprecise_dtypes=True))
            step(gp.iota(offs[:, :, :], [[1, SEG], [0, M8]], base=0, channel_multiplier=0,
                         allow_small_or_imprecise_dtypes=True))
            step(gp.iota(tnum[:, :], [[1, max(TG)]], base=0, channel_multiplier=0, allow_small_or_imprecise_dtypes=True))
            step(gp.memset(ones[:, :], 1.0))
            step(gp.memset(onesr[:, :], 1.0))
            step(gp.memset(epsb[:, :], EPS))
            step(gp.memset(zrow[:, :], 0.0))
            n = own[0]
            gp.wait_ge(pool, n)
            step(gp.affine_select(out=ident[:, :], in_=ident[:, :], compare_op=ALU.not_equal, fill=1.0, base=0,
                                  pattern=[[-1, P]], channel_multiplier=1))
            gp.wait_ge(pool, own[0])
            gp.sem_inc(consts, 1)
            n = step(gp.memset(G[:, :, :], 0.0))
            gp.wait_ge(pool, n)
            gp.wait_ge(stats0, 1)
            mean = mv[:, :, 0:1].to_broadcast([P, NT, F])
            gp.tensor_tensor(h0, xs[:, :, :], mean, ALU.subtract).then_inc(centred, 1)
            gp.wait_ge(t0_in, 16)

            def gather_chunk(n):
                l, g, c = CHUNKS[n]
                if c == 0 and l == 0:
                    gp.wait_ge(queue_ready, ORDER[0].index(g) + 1)
                if n >= SLOTS:
                    gp.wait_ge(chunk_used, n - SLOTS + 1)
                if n == HUB_SLOT:
                    gp.wait_ge(hubmask_ready, 1)
                    gp.wait_ge(pool, step(gp.memset(hub_stage.bitcast(f32), 0.0)))
                for e in range(rounds(n)):
                    src, wide = (t0, F) if l == 0 else (t1, ROW)
                    gp.indirect_dma_start(
                        G[:, slot(n) * CH + e, 0:wide], None, src,
                        bass.IndirectOffsetOnAxis(ap=idx[g][:, c * CH + e:c * CH + e + 1], axis=0),
                        bounds_check=N - 1, oob_is_err=False).then_inc(gath[slot(n)], 16)

            def gather_ends(l, g):
                last = FIRST[l, g] + NCH[l][g] - 1
                for n in range(last - RSLOTS + 1, last + 1):
                    gp.wait_ge(stored[n % RSLOTS], rstored(n))
                for t in range(TG[g]):
                    if l == 1 and g == 0 and t == 0:
                        continue
                    tile = T0G[g] + t
                    gp.indirect_dma_start(
                        A[:, tile, :], None, run[g],
                        bass.IndirectOffsetOnAxis(ap=eidx[g][:, t:t + 1], axis=0),
                        bounds_check=P * CAP[g], oob_is_err=False).then_inc(ends[l][tile // 4], 16)

            for l in range(2):
                if l:
                    gp.wait_ge(t1_in, 16 * 8)
                for nth, g in enumerate(ORDER[l]):
                    for c in range(NCH[l][g]):
                        gather_chunk(FIRST[l, g] + c)
                    if l == 0 and nth == 1:
                        gp.wait_ge(zrow_in, 16 * GROUPS)
                        gp.wait_ge(last_mask, 1)
                        gather_ends(l, ORDER[l][0])
                if l == 0:
                    for g in ORDER[0][1:]:
                        gather_ends(l, g)
            gather_ends(1, ORDER[1][0])
            gather_ends(1, ORDER[1][1])
            gather_ends(1, ORDER[1][2])

        @block.scalar
        def _(act):
            act.sem_inc(stage_used, 1)

            def convert(t):
                act.wait_ge(adj_in[t % STAGES], 16 * (t // STAGES + 1))
                if t >= STAGES:
                    act.wait_ge(mask_used, t - 1)
                nc.scalar.activation(mask[t % STAGES], stage[t % STAGES], ACT.Sign,
                                     accum_out=sgn[:, t:t + 1]).then_inc(stage_used, 1)

            act.wait_ge(adj_in[0], 16)
            src = stage[0].rearrange("p (c i) -> p c i", i=P)
            dst = mask[0].rearrange("p (c i) -> p c i", i=P)
            nc.scalar.activation(dst[:, :, 0:HUB], src[:, :, 0:HUB], ACT.Sign)
            nc.scalar.activation(dst[:, :, HUB:P], src[:, :, HUB:P], ACT.Sign,
                                 accum_out=sgn[:, 0:1]).then_inc(stage_used, 1)
            act.wait_ge(consts, 1)
            act.wait_ge(stats0, 1)
            nc.scalar.activation(sd[:, :], mv[:, :, 1], ACT.Sqrt, bias=epsb[:, 0:1]).then_inc(sd0, 1)
            convert(1)
            convert(2)
            act.wait_ge(wprep, 1)
            nc.scalar.activation(WT[:, :], ps[1][:, 3, 0:P], ACT.Copy).then_inc(wprep_c, 1)
            act.wait_ge(wprep, 2)
            nc.scalar.activation(Ws[:, F:F + 2], ps[1][:, 2, 0:2], ACT.Copy).then_inc(wprep_c, 1)
            act.wait_ge(rstd0, 1)
            act.wait_ge(centred, 1)
            for t in range(NT):
                nc.scalar.activation(h0[:, t, :], h0[:, t, :], ACT.Relu, scale=rstd[:, t:t + 1]).then_inc(h0_ready, 1)
            act.wait_ge(h0_ready, NT)
            act.dma_start(t0_v, h0).then_inc(t0_in, 16)
            act.dma_start(hub_stage, adj_v[0][0:HUB, :]).then_inc(hub_in, 16)

            def signs(first, tiles):
                done = first - 2
                with act.Fori(0, tiles // STAGES) as i:
                    for k in range(STAGES):
                        s = (2 + k) % STAGES
                        act.wait_ge(adj_in[s], i * 16 + (done // STAGES * 16 + (16 if s == 2 else 32)))
                        act.wait_ge(mask_used, i * STAGES + (done + k + 1))
                        nc.scalar.activation(mask[s], stage[s], ACT.Sign,
                                             accum_out=sgn[:, bass.ds(i * STAGES + (first + k), 1)]).then_inc(stage_used, 1)

            convert(3)
            convert(4)
            signs(5, EARLY - 8)
            act.wait_ge(hub_in, 16)
            nc.scalar.activation(hubmask, hub_stage, ACT.Sign).then_inc(hub_sign, 1)
            convert(EARLY - 3)
            act.wait_ge(hub_sign, 1)
            nc.scalar.activation(hubmask, hubmask, ACT.Abs).then_inc(hubmask_ready, 1)
            convert(EARLY - 2)
            convert(EARLY - 1)
            for b in range(8):
                act.wait_ge(h0t_ready, b + 1)
                nc.scalar.activation(HT[:, b * BANK:(b + 1) * BANK], ps[1][:, b % 4, :], ACT.Copy).then_inc(h0t_used, 1)
            signs(EARLY, NT - TURNS - EARLY)
            for n in range(TURNS):
                t = NT - TURNS + n
                convert(t)
                if t - 1 in CHUNK_TILE:
                    store_chunk(act, CHUNK_TILE.index(t - 1))

            for b in range(8 + 2):
                if b < 8:
                    act.wait_ge(rows["var"], b + 1)
                    nc.scalar.activation(sd[:, 4 * b:4 * b + 4], mv[:, 4 * b:4 * b + 4, 1], ACT.Sqrt,
                                         bias=epsb[:, 0:1]).then_inc(rows["sd"], 1)
                if 0 <= b - 1 < 8:
                    act.wait_ge(rows["turned"], b)
                    if b - 1 >= 2:
                        act.wait_ge(rows["h"], b - 2)
                    nc.scalar.activation(hTs[:, (b - 1) % 2, :], turned_rows(b - 1), ACT.Relu).then_inc(rows["relu"], 1)
                if 0 <= b - 2:
                    act.wait_ge(rows["h"], b - 1)
                    act.wait_ge(rows["scale"], b - 1)
                    for k in range(4):
                        t = 4 * (b - 2) + k
                        nc.scalar.activation(HR[:, t, 0:F], product(b - 2, k)[:, 0:F], ACT.Copy, scale=rstd[:, t:t + 1],
                                             accum_out=hsum[:, t:t + 1]).then_inc(rows["copied"], 1)

            def dense(sems, n):
                act.wait_ge(sems["score"], n + 1)
                for h in range(2):
                    act.wait_ge(sems["bc"], n * 2 + (h + 1))
                    nc.scalar.activation(U[:, h * 2048:(h + 1) * 2048], ps[0][:, :, :].rearrange("p b n -> p (b n)"),
                                         ACT.Identity, bias=dn[:, 0:1]).then_inc(sems["bc_act"], 1)
                act.wait_ge(sems["masked"], n + 1)
                nc.scalar.activation(U, U, ACT.Exp, bias=dn[:, 3:4], accum_out=dn[:, 4:5]).then_inc(sems["exp"], 1)
                for b in range(8):
                    act.wait_ge(sems["turned"], n * 8 + (b + 1))
                    act.wait_ge(sems["summed"], n * 8 + max(b, 1))
                    nc.scalar.activation(attT[:, b % 2, :], ps[0][:, b % 2, :], ACT.Copy).then_inc(sems["copied"], 1)

            def weigh(g):
                nth = ORDER[1].index(g)
                act.wait_ge(exq, nth + 1)
                c1 = CAP1[g]
                nc.scalar.activation(qv[:, 4, 0:c1], qv[:, 4, 0:c1], ACT.Exp)
                nc.scalar.activation(qv[:, 5, 0:c1], qv[:, 5, 0:c1], ACT.Exp).then_inc(exq_done, 1)
                act.wait_ge(w_ready, nth + 1)
                for e in range(c1):
                    k = K1ST[g] + e
                    if k >= 4:
                        act.wait_ge(wg_used, k - 3)
                    n = FIRST[1, g] + e // CH
                    nc.scalar.activation(WG[:, k % 4, :], G[:, slot(n) * CH + e % CH, 0:F], ACT.Copy,
                                         scale=wq[g][:, e:e + 1]).then_inc(wg_ready, 1)

            def exps(sems, order):
                for n, b in enumerate(order):
                    ts = slice(4 * b, 4 * b + 4)
                    act.wait_ge(sems["z"], n + 1)
                    nc.scalar.activation(EZ[:, ts, :], Z[:, ts, :], ACT.Relu, scale=-1.0).then_inc(sems["neg"], 1)
                    act.wait_ge(sems["neg"], n + 1)
                    nc.scalar.activation(EZ[:, ts, :], EZ[:, ts, :], ACT.Exp, scale=-1.0).then_inc(sems["ez"], 1)

            dense(ds1, 0)
            for g in ORDER[1]:
                weigh(g)
            exps(elu, ELU)
            with act.If(act.value_load(flag[0:1, 0:1], min_val=0, max_val=1) > 0):
                with act.Fori(0, NT) as t:
                    dense(gl1, t)
                exps(gelu, range(8))

        @block.tensor
        def _(pe):
            pe.wait_ge(consts2, 1)

            pe.sem_inc(mask_used, 1)
            pe.sem_inc(ds1["summed"], 1)

            def keys(n, s):
                for bank in range(BANKS):
                    pe.wait_ge(keys_used, n + (bank + 1))
                    for piece in range(2):
                        for c in (0, 2, 1, 3):
                            col = ((2 * bank + piece) * CPS + c) * P
                            at = piece * 2 * P + c % 2 * P
                            last = nc.tensor.matmul(ps[0][:, bank, at:at + P], mask[s][:, col:col + P],
                                                    diag[:, c, :], start=c < 2, stop=c >= 2)
                    last.then_inc(keys_ready, 1)
                pe.wait_ge(keys_ready, n + BANKS)
                pe.sem_inc(mask_used, 1)

            def tiles(first, count, hubs=False):
                each = 2 * STAGES if hubs else STAGES
                with pe.Fori(0, count // each) as i:
                    for k in range(each):
                        pe.wait_ge(stage_used, i * each + (first + k + 2))
                        keys(i * (each * BANKS) + (first + k) * BANKS, (2 + k) % STAGES)
                        if hubs:
                            pe.wait_ge(hub_used, i * each + (k + 1))
                            pe.sem_inc(passed_pe, 1)
                            row = identh[0:HUB, bass.ds(i * (each // 2) + k // 2, 1)].to_broadcast([HUB, P])
                            for b in range(4):
                                cols = slice(k % 2 * 2048 + b * BANK, k % 2 * 2048 + (b + 1) * BANK)
                                last = nc.tensor.matmul(ps[1][:, b, :], row, hubmask[:, cols], start=True, stop=True)
                            last.then_inc(hubp, 1)

            for t in range(2):
                pe.wait_ge(stage_used, t + 2)
                keys(t * BANKS, t)
            pe.wait_ge(w_in, 32)
            pe.wait_ge(consts, 1)
            nc.tensor.transpose(ps[1][:, 3, 0:P], Ws[:, 0:F], ident[:, :]).then_inc(wprep, 1)
            pe.wait_ge(wprep_c, 1)
            nc.tensor.matmul(ps[1][:, 2, 0:2], WT[:, :], a2[:, :], start=True, stop=True).then_inc(wprep, 1)
            tiles(2, EARLY - 2)
            pe.wait_ge(h0_ready, NT)
            for b in range(8):
                if b >= 4:
                    pe.wait_ge(h0t_used, b - 3)
                for k in range(4):
                    last = nc.tensor.transpose(ps[1][:, b % 4, k * P:(k + 1) * P], h0[:, 4 * b + k, :], ident[:, :])
                last.then_inc(h0t_ready, 1)
            pe.wait_ge(h0t_used, 8)
            pe.wait_ge(hubmask_ready, 1)
            tiles(EARLY, 2 * HUB, hubs=True)
            tiles(EARLY + 2 * HUB, NT - EARLY - 2 * HUB)
            pe.sem_inc(last_mask, 1)

            def hub_half(n, i, h, ready, used):
                pe.wait_ge(used, n + 1)
                row = identh[:, bass.ds(i, 1)].to_broadcast([P, P])
                for b in range(4):
                    last = nc.tensor.matmul(ps[h][:, b, :], row, maskn[:, h * 2048 + b * BANK:h * 2048 + (b + 1) * BANK],
                                            start=True, stop=True)
                last.then_inc(ready, 1)

            pe.wait_ge(hub_used, 2 * HUB + 1)
            nc.tensor.transpose(ps[1][:, 0, 0:P], aggT, ident[:, :]).then_inc(hub_t, 1)
            pe.wait_ge(diffs, 1)
            nc.tensor.matmul(ps[1][0:1, 1, 0:2], ones[:, 0:1], ovd[:, :], start=True, stop=True).then_inc(flag_sum, 1)

            pe.wait_ge(flag_ready, 1)
            with pe.If(pe.value_load(flag[0:1, 0:1], min_val=0, max_val=1) > 0):
                with pe.Fori(0, NT) as t:
                    pe.wait_ge(gl0["mask"], t + 1)
                    pe.sem_inc(passed_pe, 1)
                    with pe.Fori(0, P) as i:
                        r = pe.snap(t * P + i)
                        for h in range(2):
                            hub_half(r * 2 + h, i, h, gl0["p"], gl0["used"])
                    pe.wait_ge(gl0["own"], (t + 1) * P)
                    nc.tensor.transpose(ps[0][:, 0, 0:P], aggT, ident[:, :]).then_inc(gl0["t"], 1)
                    pe.wait_ge(gl0["done"], t + 2)

            for b in range(8 + 1):
                if b < 8:
                    pe.wait_ge(rows["centred"], b + 1)
                    if b >= 2:
                        pe.wait_ge(rows["relu"], b - 1)
                    for k in range(4):
                        last = nc.tensor.transpose(turned_rows(b)[:, k * P:(k + 1) * P], xn[:, b % 2, k, :], ident[:, :])
                    last.then_inc(rows["turned"], 1)
                if b >= 1:
                    pe.wait_ge(rows["relu"], b)
                    if b - 1 >= 2:
                        pe.wait_ge(rows["ready"], b - 2)
                    for k in range(4):
                        last = nc.tensor.matmul(product(b - 1, k), hTs[:, (b - 1) % 2, k * P:(k + 1) * P], Ws[:, :],
                                                start=True, stop=True)
                    last.then_inc(rows["h"], 1)

            def dense(sems, n):
                pe.wait_ge(sems["out"], n + 1)
                for h in range(2):
                    if h:
                        pe.wait_ge(sems["bc_act"], n * 2 + 1)
                        pe.wait_ge(sems["bc_dve"], n * 2 + 1)
                    for c in range(16):
                        t = 16 * h + c
                        for col, half in ((F, 0), (F + 1, 1)):
                            last = nc.tensor.matmul(ps[half][:, c // 4, c % 4 * P:(c % 4 + 1) * P],
                                                    HR[:, t, col:col + 1].to_broadcast([P, P]), ident[:, :],
                                                    start=True, stop=True)
                    last.then_inc(sems["bc"], 1)
                pe.wait_ge(sems["att"], n + 1)
                for b in range(9):
                    if b < 8:
                        if b >= 2:
                            pe.wait_ge(sems["copied"], n * 8 + (b - 1))
                        for k in range(4):
                            col = (4 * b + k) * P
                            last = nc.tensor.transpose(ps[0][:, b % 2, k * P:(k + 1) * P], T[:, col:col + P], ident[:, :])
                        last.then_inc(sems["turned"], 1)
                    if b >= 1:
                        c = b - 1
                        pe.wait_ge(sems["copied"], n * 8 + (c + 1))
                        for k in range(4):
                            last = nc.tensor.matmul(ps[1][:, 0, 0:F], attT[:, c % 2, k * P:(k + 1) * P],
                                                    HR[:, 4 * c + k, 0:F], start=(c == 0 and k == 0),
                                                    stop=(c == 7 and k == 3))
                        last.then_inc(sems["summed"], 1)

            pe.wait_ge(rows["ready"], 8)
            dense(ds1, 0)
            with pe.If(pe.value_load(flag[0:1, 0:1], min_val=0, max_val=1) > 0):
                pe.wait_ge(ds1["out"], 2)
                pe.sem_inc(gl1["summed"], 1)
                with pe.Fori(0, NT) as t:
                    dense(gl1, t)

        @block.vector
        def _(v):
            own = [0]

            def inc(ins):
                ins.then_inc(dve, 1)
                own[0] += 1
                return own[0]

            def done(ins):
                v.wait_ge(dve, inc(ins))

            v.wait_ge(consts, 1)
            for c in range(CPS):
                inc(v.tensor_scalar(diag[:, c, :], ident[:, :], kcol[:, c:c + 1], None, ALU.mult))
            inc(v.tensor_copy(identh[:, :], ident[:, :]))
            done(v.tensor_scalar(rowmask[:, :], rowmask[:, :], float(HUB), None, ALU.is_ge))
            v.sem_inc(consts2, 1)
            v.sem_inc(keys_used, 4)
            v.sem_inc(hub_used, 1)
            v.sem_inc(ds1["out"], 1)
            inc(v.memset(aggT, 0.0))
            inc(v.memset(ovs[:, :], 0.0))
            v.wait_ge(x_in, 16)
            for t in range(NT):
                inc(v.bn_stats(st6[:, t, :], xs[:, t, :]))
            v.wait_ge(dve, own[0])
            for t in range(NT):
                inc(v.bn_aggr(mv[:, t, :], st6[:, t, :]))
            v.wait_ge(dve, own[0])
            v.sem_inc(stats0, 1)
            v.wait_ge(sd0, 1)
            v.reciprocal(rstd[:, :], sd[:, :]).then_inc(rstd0, 1)

            def spread(g, out_, in_, c1):
                done(v.tensor_tensor(qe[:, 0:c1], in_, nend[g][:, :], ALU.mult))
                done(v.tensor_tensor(qe[:, 0:c1], in_, qe[:, 0:c1], ALU.subtract))
                done(v.tensor_tensor_scan(out_[:, ::-1], nend[g][:, ::-1], qe[:, 0:c1][:, ::-1], 0.0, ALU.mult, ALU.add))

            def chunk_free(n):
                v.wait_ge(gath[slot(n)], gathered(n))
                if n >= RSLOTS:
                    v.wait_ge(stored[n % RSLOTS], rstored(n - RSLOTS))

            def running(n, e):
                l, g, c = CHUNKS[n]
                at = c * CH + e
                new = R[:, n % RSLOTS, e, :]
                old = R[:, (n if e else n - 1) % RSLOTS, (e - 1) % CH, :]
                row = G[:, slot(n) * CH + e, 0:F]
                if l:
                    row = WG[:, (K1ST[g] + at) % 4, :]
                if at == 0:
                    return v.tensor_copy(new, row)
                return v.scalar_tensor_tensor(new, old, cont[g][:, at:at + 1], row, ALU.mult, ALU.add if l else ALU.max)

            def accumulate(n):
                l, g, c = CHUNKS[n]
                chunk_free(n)
                for e in range(rounds(n)):
                    if l:
                        k = K1ST[g] + c * CH + e
                        v.wait_ge(wg_ready, k + 1)
                        running(n, e).then_inc(wg_used, 1)
                        v.wait_ge(wg_used, k + 1)
                    else:
                        done(running(n, e))
                v.sem_inc(chunk_used, 1)

            def lists(t, part):
                lk, at = LIST[t], AT_LIST[t]
                k = K[:, t % 2, :]
                L_ = L[max(g for g in range(GROUPS) if T0G[g] <= t)]
                if part == 0:
                    inc(v.tensor_reduce(ovs[:, t:t + 1], k.rearrange("p (s m) -> p s m", m=M8)[:, :, M8 - 1], X, ALU.max))
                elif part == 1:
                    inc(v.tensor_tensor(k, k, offs[:, :, :].rearrange("p s m -> p (s m)"), ALU.add))
                elif part < 2 * (lk // M8) + 1:
                    r, what = divmod(part - 2, 2)
                    top = L_[:, at + r * M8:at + (r + 1) * M8]
                    if what == 0:
                        inc(v.max(top, k))
                    else:
                        inc(v.match_replace(k, top, k, 0.0))

            def search(t, chunk=None, queued=None):
                listed = t > 1 and t not in T0G
                if chunk is not None:
                    chunk_free(chunk)
                for s in range(SEG):
                    if s % 2 == 0:
                        v.wait_ge(keys_ready, t * BANKS + s // 2 + 1)
                    ins = v.max(K[:, t % 2, s * M8:(s + 1) * M8], ps[0][:, s // 2, s % 2 * 2 * P:(s % 2 + 1) * 2 * P])
                    if s % 2:
                        ins.then_inc(keys_used, 1)
                    v.wait_ge(dve, own[0])
                    if listed:
                        lists(t - 1, s)
                    if chunk is not None:
                        inc(running(chunk, s))
                    if queued is not None and queued + s < queue_rounds(0):
                        queue_round(0, queued + s)
                v.wait_ge(dve, own[0])
                if listed:
                    lists(t - 1, SEG)
                if chunk is not None:
                    v.sem_inc(chunk_used, 1)
                v.wait_ge(dve, own[0])
                v.wait_ge(keys_used, (t + 2) * BANKS)

            def finish_list(t):
                for part in range(2 * (LIST[t] // M8) + 1):
                    lists(t, part)
                    v.wait_ge(dve, own[0])

            def search0():
                per = PIECES // SEG
                for bank in range(BANKS):
                    v.wait_ge(keys_ready, bank + 1)
                    for q in range(2 * per):
                        last = v.max(K0[:, (bank * 2 * per + q) * M8:(bank * 2 * per + q + 1) * M8],
                                     ps[0][:, bank, q * (BANK // per // 2):(q + 1) * (BANK // per // 2)])
                    last.then_inc(keys_used, 1)
                v.wait_ge(keys_used, 2 * BANKS)
                done(v.tensor_scalar(K0, K0, rowmask[:, 0:1], None, ALU.mult))
                done(v.tensor_reduce(ovs[:, 0:1], K0.rearrange("p (q m) -> p q m", m=M8)[:, :, M8 - 1], X, ALU.max))
                k0 = K0.rearrange("p (s q m) -> p s q m", s=SEG, m=M8)
                done(v.tensor_tensor(k0, k0, offs[:, :, None, :].to_broadcast([P, SEG, PIECES // SEG, M8]), ALU.add))
                for r in range(LIST0 // M8):
                    done(v.max(L_first[:, r * M8:(r + 1) * M8], K0))
                    if r + 1 < LIST0 // M8:
                        done(v.match_replace(K0, L_first[:, r * M8:(r + 1) * M8], K0, 0.0))

            ov_column = iter(range(NT, 64))

            def overflow():
                n = next(ov_column)
                return ovs[:, n:n + 1]

            def queue_lists(g, part):
                start, end = (PARTS[g] + (T0G[g] + TG[g],))[part:part + 2]
                lo, hi = 0 if start == 0 else AT_LIST[start], AT_LIST[end - 1] + LIST[end - 1]
                k, li_, lw_, lf_, lh_, lsec_ = (a[:, lo:hi] for a in (L[g], li, lw, lf, lh, lsec))

                def runs(a):
                    t = max(start, 1)
                    while t < end:
                        m = t
                        while m < end and LIST[m] == LIST[t]:
                            m += 1
                        yield (slice(t - T0G[g], m - T0G[g]), m - t, LIST[t],
                               a[:, AT_LIST[t]:AT_LIST[m - 1] + LIST[t]].rearrange("p (t m) -> p t m", m=LIST[t]))
                        t = m

                for _, _, m, lists in runs(L[g]):
                    inc(v.tensor_reduce(overflow(), lists[:, :, m - 1], X, ALU.max))
                if start == 0:
                    inc(v.tensor_copy(overflow(), L[0][:, LIST0 - 1:LIST0]))
                inc(v.tensor_copy(li_, k))
                done(v.tensor_scalar(lf_, k, float(M8), None, ALU.is_ge))
                done(v.tensor_scalar(lh_, lf_, float(TILE), None, ALU.mult))
                inc(v.tensor_scalar(lw_, li_, 24, None, ALU.bitwise_and))
                for ts, n, m, lists in runs(lh):
                    inc(v.tensor_tensor(lists, lists, tnum[:, ts, None].to_broadcast([P, n, m]), ALU.mult))
                v.wait_ge(dve, own[0])
                tiles = slice(max(lo, LS[g]), hi)
                done(v.tensor_tensor(L[g][:, tiles], L[g][:, tiles], lh[:, tiles], ALU.add))
                inc(v.tensor_scalar(lsec_, lw_, 24.0, None, ALU.is_equal))
                done(v.tensor_scalar(li_, li_, TILE - M8, None, ALU.bitwise_and))
                inc(v.tensor_tensor(lf_, lf_, lsec_, ALU.add))
                done(v.tensor_scalar(lh_, li_, 8.0, 0.5, ALU.add, ALU.mult))
                for ts, _, _, lists in runs(lf):
                    inc(v.tensor_reduce(cnt[g][:, ts], lists, X, ALU.add))
                if start == 0:
                    inc(v.tensor_reduce(cnt[0][:, 0:1], lf[:, 0:LIST0], X, ALU.add))
                v.wait_ge(dve, own[0])
                inc(v.tensor_tensor(lf_, k, lh_, ALU.subtract))
                done(v.tensor_tensor(lh_, lh_, lsec_, ALU.mult))
                inc(v.tensor_tensor(k, k, lh_, ALU.subtract))
                done(v.scalar_tensor_tensor(lsec_, lf_, 8.0, lsec_, ALU.add, ALU.mult))
                second = LW[g] + part * BOTH
                done(v.max(L[g][:, second:second + BOTH], lsec_))
                done(v.tensor_copy(overflow(), L[g][:, second + BOTH - 1:second + BOTH]))

            def queue_rounds(g):
                return 2 * -(-CAP[g] // M8) - 1

            def queue_round(g, step):
                r, what = divmod(step, 2)
                k, top = L[g][:, 0:LQ[g]], Q[:, r * M8:(r + 1) * M8]
                if what == 0:
                    inc(v.max(top, k))
                else:
                    inc(v.match_replace(k, top, k, 0.0))

            def queue_indices(g):
                T, cap = TG[g], CAP[g]
                q_ = Q[:, 0:cap]
                inc(v.tensor_copy(overflow(), Q[:, cap - 1:cap]))
                inc(v.tensor_scalar(pad[:, 0:cap], q_, float(M8), float(2 * N), ALU.is_lt, ALU.mult))
                done(v.tensor_copy(qi[:, 0:cap], q_))
                inc(v.tensor_scalar(qn[:, 0:cap], qi[:, 0:cap], 2, N // 2 - 8, ALU.logical_shift_right, ALU.bitwise_and))
                inc(v.tensor_scalar(qb[:, 0:cap], qi[:, 0:cap], 16, 7, ALU.bitwise_and, ALU.logical_shift_left))
                done(v.tensor_scalar(idx[g][:, :], qi[:, 0:cap], 7, None, ALU.bitwise_and))
                done(v.tensor_tensor(qn[:, 0:cap], qn[:, 0:cap], qb[:, 0:cap], ALU.bitwise_or))
                done(v.tensor_tensor(idx[g][:, :], idx[g][:, :], qn[:, 0:cap], ALU.bitwise_or))
                done(v.tensor_tensor(idx[g][:, :], idx[g][:, :], pad[:, 0:cap], ALU.add))
                v.sem_inc(queue_ready, 1)
                inc(v.tensor_scalar(qe[:, 0:cap], q_, float(M8), None, ALU.is_lt))
                done(v.tensor_scalar(qn[:, 0:cap], qi[:, 0:cap], TILE.bit_length() - 1, None, ALU.logical_shift_right))
                done(v.tensor_tensor(tf[g][:, :], qn[:, 0:cap], qe[:, 0:cap], ALU.subtract))
                inc(v.memset(cont[g][:, 0:1], 0.0))
                inc(v.tensor_tensor(cont[g][:, 1:], tf[g][:, 1:], tf[g][:, 0:cap - 1], ALU.is_equal))
                done(v.tensor_tensor_scan(pre[:, 0:T], onesr[:, 0:T], cnt[g][:, :], 0.0, ALU.mult, ALU.add))
                done(v.tensor_tensor(ef[:, 0:T], cnt[g][:, :], pre[:, 0:T], ALU.subtract))
                done(v.tensor_scalar(ef[:, 0:T], ef[:, 0:T], pre[:, T - 1:T], None, ALU.add))
                if g == 0:
                    done(v.tensor_scalar(ovt[:, 0:1], ef[:, 1:2], float(CAP1[0]), None, ALU.is_gt))
                done(v.tensor_scalar(ef[:, 0:T], ef[:, 0:T], pcol[:, g:g + 1], None, ALU.add))
                done(v.tensor_scalar(pre[:, 0:T], cnt[g][:, :], 0.5, float(P * N), ALU.is_lt, ALU.mult))
                done(v.tensor_tensor(ef[:, 0:T], ef[:, 0:T], pre[:, 0:T], ALU.add))
                done(v.tensor_scalar(eidx[g][:, :], ef[:, 0:T], float(P * CAP[g]), None, ALU.min))

            def queue1(g):
                c1 = CAP1[g]
                inc(v.memset(nend[g][:, c1 - 1:c1], 0.0))
                inc(v.tensor_copy(nend[g][:, 0:c1 - 1], cont[g][:, 1:c1]))
                inc(v.tensor_scalar(reset[g][:, :], cont[g][:, 0:c1], BIG, -BIG, ALU.mult, ALU.add))
                done(v.tensor_tensor_scan(nq[g][:, :], cont[g][:, 0:c1], onesr[:, 0:c1], 0.0, ALU.mult, ALU.add))
                spread(g, nq[g][:, :], nq[g][:, :], c1)

            def hub_part(n):
                row, h = n // 2, n % 2
                to = aggT[:, row:row + 1]
                half = ps[1][:, :, :].rearrange("p b n -> p (b n)")
                v.wait_ge(hubp, n + 1)
                v.wait_ge(hub_used, n + 1)
                v.tensor_tensor_reduce(out=half, in0=half, in1=HT[:, h * 2048:(h + 1) * 2048], scale=1.0,
                                       scalar=hm[:, 0:1] if h else 0.0, op0=ALU.mult, op1=ALU.max,
                                       accum_out=to if h else hm[:, 0:1]).then_inc(hub_used, 1)

            def queue(g):
                for step in range(queue_rounds(g)):
                    queue_round(g, step)
                    v.wait_ge(dve, own[0])
                queue_indices(g)

            search0()
            for t in range(1, NT):
                if t in T0G:
                    finish_list(t - 1)
                    g = T0G.index(t) - 1
                    queue_lists(g, len(PARTS[g]) - 1)
                if t == T0G[2]:
                    queue(1)
                queued = (t - T0G[1]) * SEG
                if queued - SEG < queue_rounds(0) <= queued:
                    queue_indices(0)
                search(t, CHUNK_TILE.index(t) if t in CHUNK_TILE else None,
                       queued if 0 <= queued < queue_rounds(0) else None)
                if t in HUB_TILES:
                    hub_part(HUB_TILES.index(t))
                for g in range(GROUPS):
                    if t in PARTS[g][1:]:
                        queue_lists(g, PARTS[g].index(t) - 1)
            finish_list(NT - 1)
            queue_lists(GROUPS - 1, len(PARTS[GROUPS - 1]) - 1)
            queue(GROUPS - 1)

            v.wait_ge(stage_used, NT + 1)
            inc(v.tensor_reduce(ovt[:, 1:2], ovs[:, :], X, ALU.max))
            inc(v.tensor_reduce(ovt[:, 2:3], sgn[:, :], X, ALU.add))
            for g in range(GROUPS):
                inc(v.tensor_reduce(ovt[:, 3 + g:4 + g], cnt[g][:, :], X, ALU.add))
            v.wait_ge(dve, own[0])
            done(v.tensor_scalar(ovt[:, 1:2], ovt[:, 1:2], float(M8), None, ALU.is_ge))
            inc(v.tensor_tensor(ovd[:, 0:1], ovt[:, 0:1], ovt[:, 1:2], ALU.add))
            done(v.tensor_reduce(ovt[:, 3:4], ovt[:, 3:3 + GROUPS], X, ALU.add))
            done(v.tensor_tensor(ovd[:, 1:2], ovt[:, 3:4], ovt[:, 2:3], ALU.subtract))
            v.sem_inc(diffs, 1)

            def hub_half(n, h, ready, used, to):
                v.wait_ge(ready, n + 1)
                v.wait_ge(used, n + 2)
                if not isinstance(n, int):
                    v.sem_inc(passed_v, 1)
                v.tensor_tensor_reduce(out=junk[:, 0:2048], in0=ps[h][:, :, :].rearrange("p b n -> p (b n)"),
                                       in1=HT[:, h * 2048:(h + 1) * 2048], scale=1.0,
                                       scalar=hm[:, 0:1] if h else 0.0, op0=ALU.mult, op1=ALU.max,
                                       accum_out=to if h else hm[:, 0:1]).then_inc(used, 1)

            for n in range(BEHIND, L0CH):
                accumulate(n)
            v.wait_ge(flag_sum, 1)
            done(v.tensor_scalar(flagf[:, :], ps[1][0:1, 1, 0:2], 0.0, None, ALU.not_equal))
            v.tensor_tensor(flag[:, :], flagf[:, 0:1], flagf[:, 1:2], ALU.max).then_inc(flag_ready, 1)
            v.wait_ge(hub_t, 1)
            v.wait_ge(ends[0][0], 16 * 4)
            done(v.tensor_copy(A[0:HUB, 0, :], ps[1][0:HUB, 0, 0:P]))

            v.wait_ge(flag_ready, 1)
            with v.If(v.value_load(flag[0:1, 0:1], min_val=0, max_val=1) > 0):
                for b in range(8):
                    v.wait_ge(ends[0][b], 16 * 4)
                v.sem_inc(gl0["used"], 2)
                v.sem_inc(gl0["done"], 1)
                with v.Fori(0, NT) as t:
                    v.wait_ge(gl0["in"], (t + 1) * 16)
                    v.tensor_scalar(maskn, adjn, 0.0, None, ALU.not_equal).then_inc(gl0["mask"], 1)
                    with v.Fori(0, P) as i:
                        r = v.snap(t * P + i)
                        for h in range(2):
                            hub_half(r * 2 + h, h, gl0["p"], gl0["used"], hm[:, 1:2])
                        v.wait_ge(gl0["used"], r * 2 + 4)
                        v.tensor_copy(aggT[:, bass.ds(i, 1)], hm[:, 1:2]).then_inc(gl0["own"], 1)
                        v.wait_ge(gl0["own"], r + 1)
                    v.wait_ge(gl0["t"], t + 1)
                    v.tensor_copy(A[:, bass.ds(t, 1), :].rearrange("p a f -> p (a f)"),
                                  ps[0][:, 0, 0:P]).then_inc(gl0["done"], 1)
                v.wait_ge(gl0["done"], NT + 1)

            for b in range(8 + 3):
                if b < 8:
                    ts = slice(4 * b, 4 * b + 4)
                    v.wait_ge(ends[0][b], 16 * 4)
                    done(v.tensor_tensor(xs[:, ts, :], xs[:, ts, :], A[:, ts, :], ALU.add))
                    for t in range(4 * b, 4 * b + 4):
                        inc(v.bn_stats(st6[:, t, :], xs[:, t, :]))
                    v.wait_ge(dve, own[0])
                    for t in range(4 * b, 4 * b + 4):
                        inc(v.bn_aggr(mv[:, t, :], st6[:, t, :]))
                    v.wait_ge(dve, own[0])
                    v.sem_inc(rows["var"], 1)
                    if b >= 2:
                        v.wait_ge(rows["turned"], b - 1)
                    done(v.tensor_tensor(xn[:, b % 2, :, :], xs[:, ts, :], mv[:, ts, 0:1].to_broadcast([P, 4, F]),
                                         ALU.subtract))
                    v.sem_inc(rows["centred"], 1)
                if 0 <= b - 1 < 8:
                    ts = slice(4 * b - 4, 4 * b)
                    v.wait_ge(rows["sd"], b)
                    done(v.reciprocal(rstd[:, ts], sd[:, ts]))
                    v.sem_inc(rows["scale"], 1)
                if b - 3 >= 0:
                    ts = slice(4 * b - 12, 4 * b - 8)
                    v.wait_ge(rows["copied"], 4 * (b - 2))
                    for half in range(2):
                        t2 = slice(4 * b - 12 + 2 * half, 4 * b - 10 + 2 * half)
                        both = ps[1][:, 2 * ((b - 3) % 2) + half, 0:2 * (F + 2)].rearrange("p (k c) -> p k c", c=F + 2)
                        inc(v.tensor_tensor(S[:, t2], both[:, :, F], rstd[:, t2], ALU.mult))
                        inc(v.tensor_tensor(HR[:, t2, F], both[:, :, F + 1], rstd[:, t2], ALU.mult))
                    done(v.tensor_scalar(HR[:, ts, F + 1], hsum[:, ts], 0.0, None, ALU.not_equal))
                    v.sem_inc(rows["ready"], 1)

            def dense(sems, n, tile):
                steps = 14

                def mine(k, ins):
                    ins.then_inc(sems["own"], 1)
                    v.wait_ge(sems["own"], n * steps + k)

                v.tensor_copy(dn[:, 0:1], S[:, tile]).then_inc(sems["score"], 1)
                v.wait_ge(sems["in"], (n + 1) * 16)
                for h in range(2):
                    cols = slice(h * 2048, (h + 1) * 2048)
                    v.wait_ge(sems["bc"], n * 2 + (h + 1))
                    v.scalar_tensor_tensor(V[:, cols], adjn[:, cols], 0.0, ps[1][:, :, :].rearrange("p b n -> p (b n)"),
                                           ALU.is_gt, ALU.mult, accum_out=dn[:, 1 + h:2 + h]).then_inc(sems["bc_dve"], 1)
                v.wait_ge(sems["bc_dve"], n * 2 + 2)
                v.wait_ge(sems["bc_act"], n * 2 + 2)
                mine(1, v.tensor_tensor(dn[:, 5:6], dn[:, 1:2], dn[:, 2:3], ALU.add))
                mine(2, v.scalar_tensor_tensor(U, U, ALPHA, U, ALU.mult, ALU.max))
                mine(3, v.tensor_tensor(U, U, V, ALU.mult))
                mine(4, v.tensor_scalar(T, V, -NEG, NEG, ALU.mult, ALU.add))
                mine(5, v.tensor_tensor(U, U, T, ALU.add))
                mine(6, v.tensor_reduce(dn[:, 6:7], U, X, ALU.max))
                mine(7, v.tensor_scalar(dn[:, 3:4], dn[:, 6:7], -1.0, None, ALU.mult))
                v.sem_inc(sems["masked"], 1)
                v.wait_ge(sems["exp"], n + 1)
                mine(8, v.reciprocal(dn[:, 8:9], dn[:, 4:5]))
                mine(9, v.scalar_tensor_tensor(U, U, dn[:, 8:9], V, ALU.mult, ALU.mult))
                mine(10, v.tensor_reduce(dn[:, 6:7], U, X, ALU.max))
                mine(11, v.tensor_scalar(dn[:, 7:8], dn[:, 6:7], THR, None, ALU.is_gt))
                mine(12, v.tensor_tensor(dn[:, 7:8], dn[:, 7:8], dn[:, 5:6], ALU.mult))
                mine(13, v.scalar_tensor_tensor(T, U, THR, U, ALU.is_ge, ALU.mult))
                v.sem_inc(sems["att"], 1)
                v.wait_ge(sems["summed"], n * 8 + 9)
                mine(14, v.tensor_scalar(A[:, tile, :].rearrange("p a f -> p (a f)"), ps[1][:, 0, 0:F],
                                         dn[:, 7:8], None, ALU.mult))
                v.sem_inc(sems["out"], 1)

            inc(v.tensor_scalar(xs[:, :, :], xs[:, :, :], -1.0, None, ALU.add))
            dense(ds1, 0, slice(0, 1))
            v.wait_ge(dve, own[0])

            for g in ORDER[1]:
                queue1(g)
                c1 = CAP1[g]
                done(v.memset(sq[g], 0.0))
                for t in range(T0G[g] == 0, TG[g]):
                    tile = T0G[g] + t
                    done(v.tensor_scalar(qe[:, 0:c1], tf[g][:, 0:c1], float(t), S[:, tile:tile + 1], ALU.is_equal, ALU.mult))
                    done(v.tensor_tensor(sq[g], sq[g], qe[:, 0:c1], ALU.add))

            def weights(g):
                nth, c1 = ORDER[1].index(g), CAP1[g]
                D, VV, u, m, ex, exn, z, top = (qv[:, k, 0:c1] for k in range(8))
                for c in range(NCH[1][g]):
                    n = FIRST[1, g] + c
                    v.wait_ge(gath[slot(n)], gathered(n))
                    at = slice(slot(n) * CH, slot(n) * CH + rounds(n))
                    inc(v.tensor_copy(qv[:, 0, c * CH:c * CH + rounds(n)], G[:, at, F]))
                    inc(v.tensor_copy(qv[:, 1, c * CH:c * CH + rounds(n)], G[:, at, F + 1]))
                v.wait_ge(dve, own[0])
                inc(v.scalar_tensor_tensor(VV, tf[g][:, 0:c1], float(T0G[g] == 0), VV, ALU.is_ge, ALU.mult))
                done(v.tensor_tensor(u, D, sq[g], ALU.add))
                inc(v.tensor_scalar(D, nq[g][:, :], -1.0, float(N), ALU.mult, ALU.add))
                done(v.scalar_tensor_tensor(u, u, ALPHA, u, ALU.mult, ALU.max))
                inc(v.tensor_scalar(z, VV, -NEG, NEG, ALU.mult, ALU.add))
                done(v.tensor_tensor(u, u, VV, ALU.mult))
                done(v.tensor_tensor(u, u, z, ALU.add))
                done(v.tensor_tensor_scan(m, reset[g][:, :], u, -BIG, ALU.add, ALU.max))
                spread(g, m, m, c1)
                done(v.tensor_scalar(m, m, NEG, None, ALU.max))
                inc(v.tensor_tensor(ex, u, m, ALU.subtract))
                done(v.tensor_scalar(exn, m, -1.0, NEG, ALU.mult, ALU.add))
                v.sem_inc(exq, 1)
                done(v.tensor_tensor_scan(top, cont[g][:, 0:c1], VV, 0.0, ALU.mult, ALU.add))
                spread(g, wq[g], top, c1)
                v.wait_ge(exq_done, nth + 1)
                inc(v.tensor_tensor(D, D, exn, ALU.mult))
                done(v.tensor_tensor_scan(z, cont[g][:, 0:c1], ex, 0.0, ALU.mult, ALU.add))
                spread(g, z, z, c1)
                done(v.tensor_tensor(z, z, D, ALU.add))
                inc(v.tensor_tensor(ex, ex, VV, ALU.mult))
                done(v.reciprocal(z, z))
                done(v.tensor_tensor(ex, ex, z, ALU.mult))
                done(v.tensor_tensor_scan(top, cont[g][:, 0:c1], ex, 0.0, ALU.mult, ALU.max))
                spread(g, top, top, c1)
                done(v.scalar_tensor_tensor(ex, ex, THR, ex, ALU.is_ge, ALU.mult))
                done(v.scalar_tensor_tensor(ex, top, THR, ex, ALU.is_gt, ALU.mult))
                done(v.tensor_tensor(wq[g], wq[g], ex, ALU.mult))
                v.sem_inc(w_ready, 1)

            def elus(sems, order):
                for n in range(9):
                    if n < 8:
                        b = order[n]
                        ts = slice(4 * b, 4 * b + 4)
                        if sems is elu:
                            v.wait_ge(ends[1][b], 16 * (3 if b == 0 else 4))
                        v.tensor_tensor(Z[:, ts, :], HR[:, ts, 0:F], A[:, ts, :], ALU.add).then_inc(sems["z"], 1)
                    if n:
                        before = slice(4 * order[n - 1], 4 * order[n - 1] + 4)
                        v.wait_ge(sems["y"], n)
                        v.wait_ge(sems["ez"], n)
                        v.tensor_tensor(O[:, before, :], O[:, before, :], EZ[:, before, :], ALU.add).then_inc(sems["o"], 1)
                    if n < 8:
                        v.wait_ge(sems["z"], n + 1)
                        v.scalar_tensor_tensor(O[:, ts, :], Z[:, ts, :], 0.0, xs[:, ts, :], ALU.max,
                                               ALU.add).then_inc(sems["y"], 1)

            for g in ORDER[1]:
                weights(g)
                for n in range(FIRST[1, g], FIRST[1, g] + NCH[1][g]):
                    accumulate(n)
            elus(elu, ELU)

            with v.If(v.value_load(flag[0:1, 0:1], min_val=0, max_val=1) > 0):
                v.wait_ge(elu["in"], 16 * 8)
                v.sem_inc(gl1["out"], 1)
                with v.Fori(0, NT) as t:
                    dense(gl1, t, bass.ds(t, 1))
                v.wait_ge(gl1["out"], NT + 1)
                elus(gelu, range(8))


def kernel(x, adj, L1_gnn_W, L1_gnn_a):
    import numpy as np
    from concourse import bacc
    from concourse.bass_utils import run_bass_kernel_spmd

    x, adj, w, a = (np.ascontiguousarray(v) for v in (x, adj, L1_gnn_W, L1_gnn_a))
    adj_t = np.ascontiguousarray(adj.reshape(NT, P, CPS, P, SEG).transpose(0, 3, 4, 2, 1)).reshape(NT * P, N)
    a = np.ascontiguousarray(a.reshape(2, F).T)
    nc = bacc.Bacc("TRN2", target_bir_lowering=False, num_devices=1)
    arrays, args = {}, []
    for name, v in (("x", x), ("adj", adj), ("adj_t", adj_t), ("w", w), ("a", a)):
        arrays[f"in_{name}"] = v
        args.append(nc.dram_tensor(f"in_{name}", v.shape, mybir.dt.from_np(v.dtype), kind="ExternalInput").ap())
    args.append(nc.dram_tensor("out", (N, F), f32, kind="ExternalOutput").ap())
    build(nc, *args)
    return run_bass_kernel_spmd(nc, [arrays], core_ids=[0]).results[0]["out"]
```
